# Optimizing a Trainium2 kernel written in Bass

```python
import numpy as np
import jax
import jax.numpy as jnp

def _softmax(x, axis=-1):
    return jax.nn.softmax(x, axis=axis)

def _gelu(x):
    return jax.nn.gelu(x, approximate=True)

def _silu(x):
    return jax.nn.silu(x)

def _sigmoid(x):
    return jax.nn.sigmoid(x)

def _layernorm(x, axis=-1, eps=1e-05):
    m = jnp.mean(x, axis=axis, keepdims=True)
    v = jnp.var(x, axis=axis, keepdims=True)
    return (x - m) / jnp.sqrt(v + eps)

def _scatter_add(tgt, idx, src, axis=0):
    return tgt.at[idx].add(src)

def _segment_sum(src, seg, n):
    return jax.ops.segment_sum(src, seg, n)
kernel_name = 'mk_adj_resnorm_d1_adj_r2_7fc5fe'

def setup_inputs(seed: int=0):
    np.random.seed(seed)
    _w = jnp.asarray

    def _rec_inputs():
        import jax
        import jax.numpy as jnp
        _gk = jax.random.key(seed)
        x = -9.806e-05 + 1 * jax.random.normal(jax.random.fold_in(_gk, 1), (8192, 64), jnp.float32)
        _a = jax.random.bernoulli(jax.random.fold_in(_gk, 2), 0.000244141, (8192, 8192))
        _a = jnp.logical_or(_a, jnp.swapaxes(_a, -1, -2))
        _a = jnp.logical_or(_a, jnp.eye(8192, dtype=bool))
        adj = _a.astype(jnp.int32)
        return (x, adj)
    x, adj = _rec_inputs()

    def _L0_gnn_setup():
        import jax, jax.numpy as jnp
        import numpy as np
        N = 4096
        F_IN = 64
        F_OUT = 64
        NEG_SLOPE = 0.01
        MASK_FILL = -1000000000000.0
        key = jax.random.key(seed)
        k1, k2, k3, k4 = jax.random.split(key, 4)
        x = jax.random.normal(k1, (N, F_IN), dtype=jnp.float32)
        adj_matrix = jax.random.randint(k2, (N, N), 0, 2, dtype=jnp.int32)
        W = jax.random.normal(k3, (F_IN, F_OUT), dtype=jnp.float32) * (1.0 / np.sqrt(F_IN))
        a = jax.random.normal(k4, (2 * F_IN, 1), dtype=jnp.float32) * (1.0 / np.sqrt(2 * F_IN))
        return {'x': x, 'adj_matrix': adj_matrix, 'W': W, 'a': a}
    _L0_gnn_all = _L0_gnn_setup()
    _L0_gnn_in = {k: v for k, v in _L0_gnn_all.items() if k in ('W', 'a')}
    del _L0_gnn_all
    return {'x': x, 'adj': adj, 'L0_gnn_W': _L0_gnn_in['W'], 'L0_gnn_a': _L0_gnn_in['a']}

def reference(x, adj, L0_gnn_W, L0_gnn_a):
    import jax
    import jax.numpy as jnp

    def _L0_gnn_ref(x, adj_matrix, W, a):
        import jax, jax.numpy as jnp
        import numpy as np
        N = 4096
        F_IN = 64
        F_OUT = 64
        NEG_SLOPE = 0.01
        MASK_FILL = -1000000000000.0
        h = x @ W
        a1 = a[:F_OUT, 0]
        a2 = a[F_OUT:, 0]
        f1 = h @ a1
        f2 = h @ a2
        e = jax.nn.leaky_relu(f1[:, None] + f2[None, :], NEG_SLOPE)
        e = jnp.where(adj_matrix > 0, e, MASK_FILL)
        attention = jax.nn.softmax(e, axis=1)
        h_prime = attention @ h
        return jax.nn.elu(h_prime)
    x = _layernorm(x + _L0_gnn_ref(x, adj, L0_gnn_W, L0_gnn_a), axis=-1)
    return x

_drawn_inputs = setup_inputs


def setup_inputs(seed=0):
    import zlib

    import numpy as np

    out = dict(_drawn_inputs(seed))
    spreads = {}
    factors = {}
    for name, (base, spread) in spreads.items():
        noise = np.random.default_rng([zlib.crc32(name.encode()), seed]).standard_normal(out[name].shape)
        drawn = base * np.exp(spread * noise) if base else spread * noise
        out[name] = jnp.asarray(drawn.astype(out[name].dtype))
    for name, factor in factors.items():
        out[name] = (out[name] * factor).astype(out[name].dtype)
    return out
```

```python
from contextlib import ExitStack

import numpy as np

import concourse.bass as bass
from concourse import mybir

P = 128
ALU = mybir.AluOpType
ACT = mybir.ActivationFunctionType
AX_X = mybir.AxisListType.X
F32, F16, BF16, I32, U32 = mybir.dt.float32, mybir.dt.float16, mybir.dt.bfloat16, mybir.dt.int32, mybir.dt.uint32
RMAX = bass.bass_isa.ReduceOp.max

SLOPE = 0.01
EPS = 1e-5
ROWS = 1024
T = ROWS // P
COLS = 1024
B = COLS // P
HALF = T // 2
SCALE = 128.0
BY_DVE, BY_ACT, BY_POOL = (0, 4), (1, 5, 6), (2, 3, 7)


def gat_layer(nc, x, adj, W, a, out):
    N, F = x.shape
    S = N // ROWS
    NB = N // P
    CH = N // COLS
    PAIRS = CH // 2
    F1 = F + 1
    GC = 2 * F1
    PER_BANK = 512 // GC
    SPANS = [(k, min(k + PER_BANK, T)) for k in range(0, T, PER_BANK)]
    AB = len(SPANS)
    STEPS = 2 * B
    assert F == 64 and N % ROWS == 0 and CH % 2 == 0 and 2 * AB + 2 == 8

    x_tiles = x.rearrange("(s t p) f -> s p t f", p=P, t=T)
    out_tiles = out.rearrange("(s t p) f -> s p t f", p=P, t=T)
    adj_halves = adj.rearrange("(s h t p) (c w) -> s c h p t w", p=P, t=HALF, h=2, w=COLS)

    LIMITS = (6.0, 448.0 ** 2, NB * F / 64.0)

    with ExitStack() as ctx:
        def sb(name, shape, dt):
            return ctx.enter_context(nc.sbuf_tensor(name, shape, dt))

        def sem(name):
            return ctx.enter_context(nc.semaphore(name))

        acc = ctx.enter_context(nc.psum_tensor("acc", [P, 2 * AB, 512], F32))
        turned = ctx.enter_context(nc.psum_tensor("turned", [P, 2, ROWS], BF16))

        ring = sb("ring", [P, 4, HALF, COLS], I32)
        marks = sb("marks", [P, 2, T, COLS], BF16)
        signs = sb("signs", [P, 2, ROWS], BF16)
        pos = sb("pos", [P, 4, ROWS], BF16)
        neg = sb("neg", [P, 4, ROWS], BF16)
        f1row = sb("f1row", [P, S, T // 2, 2, P], F32)
        parts = sb("parts", [P, NB, 2, GC], F16)
        h = sb("h", [P, NB, F1], F32)
        f12 = sb("f12", [P, NB, 2], F32)
        a_in = sb("a_in", [F, 2], F32)
        ident16 = sb("ident16", [P, P], BF16)
        zeros = sb("zeros", [P, P], BF16)
        ones = sb("ones", [P, P], F32)
        eps = sb("eps", [P, 1], F32)
        ab = sb("ab", [P, 2, NB, 1], F32)
        stat = sb("stat", [P, 1], F32)
        bound = sb("bound", [P, 3], F32)
        bounds = sb("bounds", [P, 3], F32)
        beyond = sb("beyond", [P, 2], F32)
        flag = sb("flag", [P, 1], I32)
        fmax = sb("fmax", [P, 3], F32)
        hcol = sb("hcol", [P, F1], F32)
        hsum = sb("hsum", [P, 1, F1], F32)
        sums = sb("sums", [P, 2, T, F1], F32)
        xin = sb("xin", [P, T, F], F32)
        dev = sb("dev", [P, T, F], F32)
        tiny = sb("tiny", [P, 6, T, 1], F32)

        def inside(place, start, *shape):
            size = int(np.prod(shape[1:]))
            flat = place[0:shape[0]].rearrange("p t f -> p (t f)")[:, start:start + size]
            names = "abc"[:len(shape) - 1]
            split = f"p ({' '.join(names)}) -> p {' '.join(names)}"
            return flat.rearrange(split, **dict(zip(names[1:], shape[2:]))), start + size

        wa1, end = inside(xin, 0, P, 2, P)
        wt2, end = inside(xin, end, F, 2, F)
        q, end = inside(xin, end, P, 2, NB)
        wblk, end = inside(dev, 0, P, 2, F + 2)
        w_in, end = inside(dev, end, P, F)
        ident, end = inside(dev, end, P, P)
        z, end = inside(dev, end, P, 2, NB)
        wide = sums[:].rearrange("p k t f -> p (k t) f")
        alone, recip, mean, var, root, rstd = (tiny[:, i] for i in range(6))
        x_all = f1row[:, S // 2:].rearrange("p s u e w -> p (s u e w)").rearrange("p (t f) -> p t f", f=F)
        xT = parts[:, NB // 2:].rearrange("p t k c -> p (t k c)")[:, 0:NB * F * 2].bitcast(F32) \
            .rearrange("p (u w) -> p u w", w=P)


        x_loaded, w_loaded, a_loaded = sem("x_loaded"), sem("w_loaded"), sem("a_loaded")
        adj_loaded = [sem(f"adj_loaded{i}") for i in range(4)]
        marked = {e: sem(f"marked_{e}") for e in ("dve", "act", "pool")}
        consts_ready, w_placed = sem("consts_ready"), sem("w_placed")
        product_made = sem("product_made")
        product_taken = {"dve": sem("product_taken_dve"), "act": sem("product_taken_act")}
        stat_ready, fmax_ready, shift_ready = sem("stat_ready"), sem("fmax_ready"), sem("shift_ready")
        q_ready, z_ready, ab_ready = sem("q_ready"), sem("z_ready"), sem("ab_ready")
        parts_ready, hcol_ready = sem("parts_ready"), sem("hcol_ready")
        turned_done, signs_made = sem("turned_done"), sem("signs_made")
        pos_made, neg_made, main_done = sem("pos_made"), sem("neg_made"), sem("main_done")
        acc_taken, agg_ready, recip_ready = sem("acc_taken"), sem("agg_ready"), sem("recip_ready")
        xin_loaded, below_ready, exp_ready = sem("xin_loaded"), sem("below_ready"), sem("exp_ready")
        y_ready, var_ready, root_ready = sem("y_ready"), sem("var_ready"), sem("root_ready")
        rstd_ready, out_ready, out_stored = sem("rstd_ready"), sem("out_ready"), sem("out_stored")
        bound_ready, bounds_ready, flag_ready = sem("bound_ready"), sem("bounds_ready"), sem("flag_ready")
        g_adj_loaded, g_x_loaded, g_stored, g_ident_ready, g_row_made, g_row_taken = (
            sem(n) for n in ("g_adj_loaded", "g_x_loaded", "g_stored", "g_ident_ready", "g_row_made", "g_row_taken"))
        g_scored, g_masked, g_weighted, g_turns, g_copied, g_added = (
            sem(n) for n in ("g_scored", "g_masked", "g_weighted", "g_turns", "g_copied", "g_added"))
        g_below_ready, g_exp_ready, g_var_ready, g_root_ready, g_out_ready, g_dve_own, g_act_own = (
            sem(n) for n in ("g_below_ready", "g_exp_ready", "g_var_ready", "g_root_ready", "g_out_ready",
                             "g_dve_own", "g_act_own"))
        dve_own, act_own, pool_own = sem("dve_own"), sem("act_own"), sem("pool_own")
        var_chain, root_chain, high_taken = sem("var_chain"), sem("root_chain"), sem("high_taken")

        passed = {nc.sync: sem("passed_sync"), nc.scalar: sem("passed_scalar"), nc.vector: sem("passed_vector"),
                  nc.gpsimd: sem("passed_gpsimd"), nc.tensor: sem("passed_tensor")}

        def hold(eng, signal, value):
            eng.wait_ge(signal, value).then_inc(passed[eng], 1)

        def at(kind, k):
            return acc[:, AB * kind + k // PER_BANK, GC * (k % PER_BANK):GC * (k % PER_BANK + 1)]

        products = [("wt", 0), ("wa", 0)] + [("xt", g) for g in range(NB // 8)] \
            + [("h", g) for g in range(NB // 4)] + [("f1", g) for g in range(2 * S)] + [("hsum", 0)]
        number = {p: n for n, p in enumerate(products)}
        BANKS = 2 * AB

        def taken(eng, n):
            eng.wait_ge(product_taken["act" if n % 2 else "dve"], n // 2 + 1)

        def take_products(eng, engine, copy):
            for n, (what, g) in enumerate(products):
                if ("act" if n % 2 else "dve") != engine:
                    continue
                bank = acc[:, n % BANKS]
                eng.wait_ge(product_made, n + 1)
                if what == "wt":
                    copy(wt2[:, 0], bank[0:F, 0:F])
                    last = copy(wt2[:, 1], bank[0:F, 0:F])
                elif what == "wa":
                    for r in range(2):
                        rows = slice(F * r, F * r + F)
                        copy(wblk[rows, r, F:F + 2], bank[rows, 0:2])
                        last = copy(wa1[rows, r, :], bank[rows, 0:1].to_broadcast([F, P]))
                elif what == "xt":
                    last = copy(xT[:, 4 * g:4 * g + 4], bank.rearrange("p (u w) -> p u w", w=P))
                elif what == "h":
                    rows = bank[:, 0:4 * (F + 2)].rearrange("p (t f) -> p t f", f=F + 2)
                    copy(h[:, 4 * g:4 * g + 4, 0:F], rows[:, :, 0:F])
                    last = copy(f12[:, 4 * g:4 * g + 4, :], rows[:, :, F:F + 2])
                elif what == "f1":
                    last = copy(f1row[:, g // 2, :, g % 2, :], bank.rearrange("p (u w) -> p u w", w=P))
                else:
                    last = copy(hsum[:, 0], bank[:, 0:F1])
                last.then_inc(product_taken[engine], 1)
                yield what, g

        def edges_marked(eng, chunks):
            hold(eng, marked["dve"], chunks * len(BY_DVE))
            hold(eng, marked["act"], chunks * len(BY_ACT))
            hold(eng, marked["pool"], chunks * len(BY_POOL))

        def may_mark(eng, s, c, k):
            hold(eng, adj_loaded[2 * (c % 2) + k // HALF], (s * CH + c - c % 2) * 8 + 16)
            if not (isinstance(s, int) and s == 0 and c < 2):
                hold(eng, turned_done, (s * CH + c - 1) * B)

        def tile_of(c, k):
            return ring[:, 2 * (c % 2) + k // HALF, k % HALF], marks[:, c % 2, k]

        def over_supers(eng, one):
            one(0, 0, False)
            one(1, 1, False)
            with eng.Fori(2, S - 1) as s:
                one(s, 2, False)
            one(S - 1, 2, True)

        halves = ring[:].rearrange("p (a b) t w -> p a (b t w)", a=2)
        g_adj, g_scores = halves[:, 0], halves[:, 1].bitcast(F32)
        g_f2row = marks[:].rearrange("p a t w -> p (a t w)").bitcast(F32)
        g_mask = pos[:].rearrange("p a w -> p (a w)").bitcast(F32)
        g_turned = neg[:].rearrange("p a w -> p (a w)").bitcast(F32).rearrange("p (g w) -> p g w", g=4)
        g_ident = signs[:, 0, 0:2 * P].bitcast(F32)
        g_h, g_below, g_sq, g_dev, g_x = sums[:, 0, 0, 0:F], sums[:, 0, 1, 0:F], sums[:, 0, 2, 0:F], dev[:, 0], xin[:, 0]
        g_max, g_sum, g_recip, g_mean, g_var, g_root, g_rstd = (sums[:, 1, i, 0:1] for i in range(7))

        num, below = sums[:, 0, :, 0:F], sums[:, 1, :, 0:F]

        def where_needed(eng, general):
            eng.wait_ge(flag_ready, 1)
            with eng.If(eng.value_load(flag[0:1, 0:1], min_val=0, max_val=1) > 0):
                general()

        block = ctx.enter_context(nc.Block())

        @block.sync
        def _(sp):
            def load(s, c):
                edges_marked(sp, s * CH + c - 1)
                for half in range(2):
                    src = adj_halves[bass.ds(s, 1), c, half].rearrange("s p t w -> p (s t) w")
                    sp.dma_start(ring[:, 2 * (c % 2) + half], src).then_inc(adj_loaded[2 * (c % 2) + half], 16)

            def rows_in(s):
                hold(sp, var_ready, s)
                sp.dma_start(xin[:], x_tiles[bass.ds(s, 1)].rearrange("s p t f -> p (s t) f")).then_inc(xin_loaded, 16)

            def rows_out(s):
                hold(sp, out_ready, s + 1)
                sp.dma_start(out_tiles[bass.ds(s, 1)].rearrange("s p t f -> p (s t) f"), dev[:]).then_inc(out_stored, 16)

            sp.dma_start(x_all, x.rearrange("(t p) f -> p t f", p=P)).then_inc(x_loaded, 16)
            sp.dma_start(w_in[0:F, :], W).then_inc(w_loaded, 16)
            sp.dma_start(w_in[F:2 * F, :], W).then_inc(w_loaded, 16)
            with nc.allow_non_contiguous_dma(reason="128 numbers"):
                sp.dma_start(a_in[:, :], a.rearrange("(c f) o -> f (c o)", c=2)).then_inc(a_loaded, 16)
            for c in range(2):
                for half in range(2):
                    sp.dma_start(ring[:, 2 * c + half], adj_halves[0, c, half]).then_inc(adj_loaded[2 * c + half], 16)

            def one(s, earlier, last):
                for c in range(CH):
                    if earlier or c > 1:
                        load(s, c)
                    if c == 2 and earlier:
                        rows_in(s - 1)
                    if c == 3 and earlier == 2:
                        rows_out(s - 2)

            over_supers(sp, one)
            rows_in(S - 1)
            rows_out(S - 2)
            rows_out(S - 1)
            sp.wait_ge(out_stored, 16 * S)

            def general():
                with sp.Fori(0, NB) as t:
                    sp.dma_start(g_adj, adj[bass.ds(t * P, P), :]).then_inc(g_adj_loaded, 16)
                    sp.dma_start(g_x, x[bass.ds(t * P, P), :]).then_inc(g_x_loaded, 16)
                    hold(sp, g_out_ready, t + 1)
                    sp.dma_start(out[bass.ds(t * P, P), :], g_dev).then_inc(g_stored, 16)
                    hold(sp, g_stored, t * 16 + 16)

            where_needed(sp, general)

        @block.gpsimd
        def _(pool):
            nc.gpsimd.memset(ident, 0.0).then_inc(pool_own, 1)
            pool.wait_ge(pool_own, 1)
            nc.gpsimd.affine_select(out=ident, in_=ident, compare_op=ALU.not_equal, fill=1.0, base=0,
                                    pattern=[[-1, P]], channel_multiplier=1).then_inc(pool_own, 1)
            pool.wait_ge(pool_own, 2)
            nc.gpsimd.tensor_copy(ident16[:], ident)
            nc.gpsimd.memset(wblk, 0.0)
            nc.gpsimd.memset(wa1, 0.0)
            nc.gpsimd.memset(ones[:], 1.0)
            nc.gpsimd.memset(eps[:], EPS)
            nc.gpsimd.memset(zeros[:].bitcast(F32), 0.0)
            nc.gpsimd.memset(h[:, :, F:F1], 1.0).then_inc(consts_ready, 1)

            def mark(s, c):
                for k in BY_POOL:
                    may_mark(pool, s, c, k)
                    src, dst = tile_of(c, k)
                    nc.gpsimd.tensor_scalar(dst, src, 0, None, ALU.is_le).then_inc(marked["pool"], 1)

            mark(0, 0)
            pool.wait_ge(stat_ready, 1)
            nc.gpsimd.partition_all_reduce(fmax[:, 0:1], stat[:], P, RMAX).then_inc(fmax_ready, 1)

            OWN = 7

            def linked(s, n, ins):
                ins.then_inc(pool_own, 1)
                hold(pool, pool_own, s * OWN + (2 + n))

            def aggregate(s):
                hold(pool, acc_taken, s * BANKS + BANKS)
                pool.wait_ge(ab_ready, 1)
                for kind in range(2):
                    last = nc.gpsimd.tensor_tensor(sums[:, kind], sums[:, kind],
                                                   ab[:, kind, bass.ds(s * T, T)].to_broadcast([P, T, F1]), ALU.mult)
                linked(s, 1, last)
                linked(s, 2, nc.gpsimd.tensor_tensor(sums[:, 0], sums[:, 0], sums[:, 1], ALU.add))
                linked(s, 3, nc.gpsimd.tensor_scalar(alone, sums[:, 0, :, F:F1], 0.0, None, ALU.is_le))
                if isinstance(s, int) and s == 0:
                    taken(pool, number[("hsum", 0)])
                linked(s, 4, nc.gpsimd.tensor_tensor(sums[:, 1], hsum[:].to_broadcast([P, T, F1]),
                                                     alone.to_broadcast([P, T, F1]), ALU.mult))
                nc.gpsimd.tensor_tensor(sums[:, 0], sums[:, 0], sums[:, 1], ALU.add).then_inc(agg_ready, 1)

            def average(s):
                hold(pool, recip_ready, s + 1)
                linked(s, 5, nc.gpsimd.tensor_tensor(num, num, recip.to_broadcast([P, T, F]), ALU.mult))
                nc.gpsimd.tensor_scalar(below, num, 0.0, None, ALU.min).then_inc(below_ready, 1)
                linked(s, 6, nc.gpsimd.tensor_scalar(num, num, 0.0, -1.0, ALU.max, ALU.add))
                hold(pool, xin_loaded, s * 16 + 16)
                linked(s, 7, nc.gpsimd.tensor_tensor(xin[:], xin[:], num, ALU.add))

            def residual(s):
                hold(pool, exp_ready, s + 1)
                nc.gpsimd.tensor_tensor(xin[:], xin[:], below, ALU.add).then_inc(y_ready, 1)

            def normed(s):
                hold(pool, rstd_ready, s + 1)
                nc.gpsimd.tensor_tensor(dev[:], dev[:], rstd.to_broadcast([P, T, F]), ALU.mult).then_inc(out_ready, 1)

            def one(s, earlier, last):
                for c in range(CH):
                    if not (last and c == CH - 1):
                        mark(s + (c + 1) // CH, (c + 1) % CH)
                    if c == 1 and earlier == 2:
                        normed(s - 2)
                    if c == 1 and earlier:
                        aggregate(s - 1)
                    if c == 3 and earlier:
                        average(s - 1)
                    if c == 5 and earlier:
                        residual(s - 1)

            pool.wait_ge(bound_ready, 2)
            nc.gpsimd.partition_all_reduce(bounds[:], bound[:], P, RMAX).then_inc(bounds_ready, 1)
            over_supers(pool, one)
            normed(S - 2)
            aggregate(S - 1)
            average(S - 1)
            residual(S - 1)
            normed(S - 1)

            def general():
                pool.wait_ge(g_adj_loaded, 16)
                nc.gpsimd.memset(g_ident, 0.0).then_inc(g_ident_ready, 1)
                pool.wait_ge(g_ident_ready, 1)
                nc.gpsimd.affine_select(out=g_ident, in_=g_ident, compare_op=ALU.not_equal, fill=1.0, base=0,
                                        pattern=[[-1, P]], channel_multiplier=1).then_inc(g_ident_ready, 1)

            where_needed(pool, general)

        @block.scalar
        def _(act):
            def copy(dst, src):
                return nc.scalar.copy(dst, src)

            act.wait_ge(consts_ready, 1)
            act.wait_ge(w_loaded, 32)
            for r in range(2):
                rows = slice(F * r, F * r + F)
                last = copy(wblk[rows, r, 0:F], w_in[rows, :])
            last.then_inc(w_placed, 1)
            for _ in take_products(act, "act", copy):
                pass

            def mark(s, c, k):
                may_mark(act, s, c, k)
                src, dst = tile_of(c, k)
                nc.scalar.activation(dst, src, ACT.Relu, bias=ones[:, 0:1], scale=-1.0).then_inc(marked["act"], 1)

            for k in BY_ACT:
                mark(0, 0, k)
            act.wait_ge(shift_ready, 1)
            nc.scalar.activation(q[:, 0], f12[:, :, 1], ACT.Exp, bias=fmax[:, 1:2])
            nc.scalar.activation(q[:, 1], f12[:, :, 1], ACT.Exp, bias=fmax[:, 2:3], scale=SLOPE).then_inc(q_ready, 1)
            act.wait_ge(z_ready, 1)
            nc.scalar.activation(ab[:, :, :, 0], z, ACT.Exp).then_inc(ab_ready, 1)

            squares = pos[:].rearrange("p a w -> p (a w)").rearrange("p (t f) -> p t f", f=F)
            nc.scalar.activation(squares, h[:, :, 0:F], ACT.Square, accum_out=bound[:, 2:3]).then_inc(bound_ready, 1)

            def sign(s, jb):
                n = s * NB + jb
                if not (isinstance(s, int) and s == 0 and jb < 2):
                    hold(act, pos_made, n - 1)
                row = f1row[:, bass.ds(s, 1)].rearrange("p s u e w -> p (s u e w)")
                nc.scalar.activation(signs[:, jb % 2], row, ACT.Sign, bias=f12[:, jb, 1:2]).then_inc(signs_made, 1)

            def exp_below(s):
                act.wait_ge(below_ready, s + 1)
                nc.scalar.activation(below, below, ACT.Exp).then_inc(exp_ready, 1)

            def inverse_root(s):
                act.wait_ge(var_ready, s + 1)
                nc.scalar.activation(root, var, ACT.Ln, bias=eps[:], scale=1.0 / F).then_inc(act_own, 1)
                act.wait_ge(act_own, s + 1)
                nc.scalar.activation(root, root, ACT.Exp, scale=-0.5).then_inc(root_ready, 1)

            def one(s, earlier, last):
                for c in range(CH):
                    for q_ in range(B):
                        sign(s, c * B + q_)
                        ahead = c + 1
                        if q_ in ACT_AT and not (last and ahead == CH):
                            mark(s + ahead // CH, ahead % CH, BY_ACT[ACT_AT.index(q_)])
                    if c == 4 and earlier:
                        exp_below(s - 1)
                    if c == 7 and earlier:
                        inverse_root(s - 1)

            ACT_AT = [1, 3, 5, 7][:len(BY_ACT)]
            over_supers(act, one)
            exp_below(S - 1)
            inverse_root(S - 1)

            def general():
                act.wait_ge(g_row_taken, NB // 4)
                with act.Fori(0, NB) as t:
                    hold(act, g_adj_loaded, t * 16 + 16)
                    nc.scalar.activation(g_scores, g_f2row, ACT.Identity, bias=f12[:, bass.ds(t, 1), 0:1]
                                         .rearrange("p t o -> p (t o)")).then_inc(g_scored, 1)
                    hold(act, g_masked, t + 1)
                    nc.scalar.activation(g_scores, g_scores, ACT.Exp, bias=g_max, accum_out=g_sum).then_inc(g_weighted, 1)
                    hold(act, g_below_ready, t + 1)
                    nc.scalar.activation(g_below, g_below, ACT.Exp).then_inc(g_exp_ready, 1)
                    hold(act, g_var_ready, t + 1)
                    nc.scalar.activation(g_root, g_var, ACT.Ln, bias=eps[:], scale=1.0 / F).then_inc(g_act_own, 1)
                    hold(act, g_act_own, t + 1)
                    nc.scalar.activation(g_root, g_root, ACT.Exp, scale=-0.5).then_inc(g_root_ready, 1)

            where_needed(act, general)

        @block.vector
        def _(dve):
            own = [0]

            def link(ins):
                own[0] += 1
                ins.then_inc(dve_own, 1)
                dve.wait_ge(dve_own, own[0])

            def copy(dst, src):
                return nc.vector.tensor_copy(dst, src)

            def mark(s, c, k):
                may_mark(dve, s, c, k)
                src, dst = tile_of(c, k)
                nc.vector.tensor_scalar(dst, src, 0, None, ALU.is_le).then_inc(marked["dve"], 1)

            take = take_products(dve, "dve", copy)
            for what, g in take:
                if what == "h" and g >= NB // 4 - 2:
                    break
            for g in (NB // 4 - 2, NB // 4 - 1):
                taken(dve, number[("h", g)])
            nc.vector.reduce_max(stat[:], f12[:, :, 1], AX_X).then_inc(stat_ready, 1)
            nc.vector.tensor_reduce(bound[:, 1:2], f12[:, :, 1], AX_X, ALU.min)
            dve.wait_ge(stat_ready, 1)
            link(nc.vector.tensor_copy(bound[:, 0:1], stat[:]))
            nc.vector.tensor_scalar(bound[:, 1:2], bound[:, 1:2], -1.0, None, ALU.mult).then_inc(bound_ready, 1)
            for what, g in take:
                if what == "f1" and g >= 2 * S - 2:
                    break
            dve.wait_ge(fmax_ready, 1)
            nc.vector.tensor_scalar(fmax[:, 1:2], fmax[:, 0:1], -1.0, None, ALU.mult)
            nc.vector.tensor_scalar(fmax[:, 2:3], fmax[:, 0:1], -SLOPE, None, ALU.mult).then_inc(shift_ready, 1)
            link(nc.vector.tensor_scalar(z[:, 0], f12[:, :, 0], fmax[:, 0:1], 1.0 - SLOPE, ALU.add, ALU.mult))
            link(nc.vector.tensor_scalar(z[:, 1], z[:, 0], -1.0, 0.0, ALU.mult, ALU.min))
            nc.vector.tensor_scalar(z[:, 0], z[:, 0], 0.0, None, ALU.min).then_inc(z_ready, 1)
            for k in BY_DVE:
                mark(0, 0, k)
            dve.wait_ge(q_ready, 1)
            for g in range(4):
                blocks = slice(16 * g, 16 * g + 16)
                if g == 2:
                    dve.wait_ge(product_made, number[("hsum", 0)])
                for kind in range(2):
                    w = q[:, kind, blocks].rearrange("p (t o) -> p t o", o=1).to_broadcast([P, 16, F1])
                    high, low = parts[:, blocks, kind, 0:F1], parts[:, blocks, kind, F1:GC]
                    link(nc.vector.scalar_tensor_tensor(wide, h[:, blocks], SCALE, w, ALU.mult, ALU.mult))
                    link(nc.vector.tensor_copy(high, wide))
                    last = nc.vector.tensor_tensor(low, wide, high, ALU.subtract)
                    if kind == 0:
                        link(last)
                last.then_inc(parts_ready, 1)
                dve.wait_ge(parts_ready, g + 1)
            nc.vector.tensor_reduce(hcol[:], h[:].rearrange("p t f -> p f t"), AX_X, ALU.add).then_inc(hcol_ready, 1)
            for _ in take:
                pass

            def step(s, jb):
                n = s * NB + jb
                dve.wait_ge(turned_done, n + 1)
                dve.wait_ge(signs_made, n + 1)
                if not (isinstance(s, int) and s == 0 and jb < 4):
                    dve.wait_ge(main_done, n - 3)
                nc.vector.tensor_tensor(pos[:, jb % 4], signs[:, jb % 2], turned[:, jb % 2], ALU.is_gt) \
                    .then_inc(pos_made, 1)
                dve.wait_ge(pos_made, n + 1)
                nc.vector.tensor_tensor(neg[:, jb % 4], pos[:, jb % 4], turned[:, jb % 2], ALU.is_equal) \
                    .then_inc(neg_made, 1)

            def take_sums(s):
                dve.wait_ge(main_done, s * NB + NB)
                banks = [(kind, b, k0, k1) for kind in range(2) for b, (k0, k1) in enumerate(SPANS)]
                for i in range(BANKS + 1):
                    if i < BANKS:
                        kind, b, k0, k1 = banks[i]
                        high = acc[:, i, 0:GC * (k1 - k0)].rearrange("p (k c) -> p k c", c=GC)[:, :, 0:F1]
                        copy(sums[:, kind, k0:k1], high).then_inc(high_taken, 1)
                    if i:
                        kind, b, k0, k1 = banks[i - 1]
                        low = acc[:, i - 1, 0:GC * (k1 - k0)].rearrange("p (k c) -> p k c", c=GC)[:, :, F1:GC]
                        dve.wait_ge(high_taken, s * BANKS + i)
                        nc.vector.tensor_tensor(sums[:, kind, k0:k1], sums[:, kind, k0:k1], low, ALU.add) \
                            .then_inc(acc_taken, 1)

            def reciprocal(s):
                dve.wait_ge(agg_ready, s + 1)
                nc.vector.reciprocal(recip, sums[:, 0, :, F:F1]).then_inc(recip_ready, 1)

            def linked(chain, value, ins):
                ins.then_inc(chain, 1)
                dve.wait_ge(chain, value)

            def variance(s):
                dve.wait_ge(y_ready, s + 1)
                linked(var_chain, s * 4 + 1, nc.vector.tensor_reduce(mean, xin[:], AX_X, ALU.add))
                linked(var_chain, s * 4 + 2, nc.vector.tensor_scalar(mean, mean, -1.0 / F, None, ALU.mult))
                if not (isinstance(s, int) and s == 0):
                    dve.wait_ge(out_stored, s * 16)
                linked(var_chain, s * 4 + 3, nc.vector.tensor_tensor(dev[:], xin[:], mean.to_broadcast([P, T, F]), ALU.add))
                linked(var_chain, s * 4 + 4, nc.vector.tensor_tensor(below, dev[:], dev[:], ALU.mult))
                nc.vector.tensor_reduce(var, below, AX_X, ALU.add).then_inc(var_ready, 1)

            def refine(s):
                dve.wait_ge(root_ready, s + 1)
                linked(root_chain, s * 4 + 1, nc.vector.tensor_scalar(mean, var, 1.0 / F, EPS, ALU.mult, ALU.add))
                linked(root_chain, s * 4 + 2, nc.vector.tensor_tensor(rstd, root, root, ALU.mult))
                linked(root_chain, s * 4 + 3, nc.vector.tensor_tensor(rstd, rstd, mean, ALU.mult))
                linked(root_chain, s * 4 + 4, nc.vector.tensor_scalar(rstd, rstd, -0.5, 1.5, ALU.mult, ALU.add))
                nc.vector.tensor_tensor(rstd, rstd, root, ALU.mult).then_inc(rstd_ready, 1)

            DVE_AT = [2, 5]

            def one(s, earlier, last):
                for c in range(CH):
                    for q_ in range(B):
                        step(s, c * B + q_)
                        ahead = c + 1
                        if q_ in DVE_AT and not (last and ahead == CH):
                            mark(s + ahead // CH, ahead % CH, BY_DVE[DVE_AT.index(q_)])
                    if c == 0 and earlier == 2:
                        refine(s - 2)
                    if c == 2 and earlier:
                        reciprocal(s - 1)
                    if c == 6 and earlier:
                        variance(s - 1)
                take_sums(s)

            over_supers(dve, one)
            dve.wait_ge(bounds_ready, 1)
            link(nc.vector.tensor_tensor(beyond[:, 0:1], bounds[:, 0:1], bounds[:, 1:2], ALU.add))
            link(nc.vector.tensor_scalar(beyond[:, 0:1], beyond[:, 0:1], LIMITS[0], None, ALU.is_le))
            link(nc.vector.tensor_scalar(beyond[:, 1:2], bounds[:, 2:3], LIMITS[1], None, ALU.is_le))
            link(nc.vector.tensor_tensor(beyond[:, 0:1], beyond[:, 0:1], beyond[:, 1:2], ALU.mult))
            link(nc.vector.tensor_scalar(beyond[:, 1:2], bounds[:, 2:3], LIMITS[2], None, ALU.is_ge))
            link(nc.vector.tensor_tensor(beyond[:, 0:1], beyond[:, 0:1], beyond[:, 1:2], ALU.mult))
            nc.vector.tensor_scalar(flag[:], beyond[:, 0:1], 0.0, None, ALU.is_equal).then_inc(flag_ready, 1)
            refine(S - 2)
            reciprocal(S - 1)
            variance(S - 1)
            refine(S - 1)

            def general():
                links = [0]

                def own(t, ins):
                    links[0] += 1
                    ins.then_inc(g_dve_own, 1)
                    dve.wait_ge(g_dve_own, t * OWN + links[0])

                for g in range(NB // 4):
                    dve.wait_ge(g_row_made, g + 1)
                    copy(g_f2row[:, 4 * P * g:4 * P * (g + 1)], acc[:, g % 4]).then_inc(g_row_taken, 1)

                QUARTER = N // 4
                OWN = 3 * 4 + 15
                with dve.Fori(0, NB) as t:
                    dve.wait_ge(g_adj_loaded, t * 16 + 16)
                    dve.wait_ge(g_x_loaded, t * 16 + 16)
                    dve.wait_ge(g_scored, t + 1)
                    for i in range(4):
                        span = slice(QUARTER * i, QUARTER * (i + 1))
                        own(t, nc.vector.scalar_tensor_tensor(g_scores[:, span], g_scores[:, span], SLOPE,
                                                                      g_scores[:, span], ALU.mult, ALU.max))
                        nc.vector.scalar_tensor_tensor(g_scores[:, span], g_adj[:, span], 0.0, g_scores[:, span],
                                                       ALU.is_gt, ALU.mult)
                        own(t, nc.vector.tensor_scalar(g_mask, g_adj[:, span], 0.0, -1e12, ALU.is_le, ALU.mult))
                        own(t, nc.vector.tensor_tensor(g_scores[:, span], g_scores[:, span], g_mask, ALU.add))
                    own(t, nc.vector.reduce_max(g_max, g_scores, AX_X))
                    nc.vector.tensor_scalar(g_max, g_max, -1.0, None, ALU.mult).then_inc(g_masked, 1)
                    for g in range(NB // 4):
                        dve.wait_ge(g_turns, t * (NB // 4) + (g + 1))
                        copy(g_turned[:, g % 4], acc[:, g % 4]).then_inc(g_copied, 1)
                    dve.wait_ge(g_added, t + 1)
                    own(t, nc.vector.reciprocal(g_recip, g_sum))
                    own(t, nc.vector.tensor_scalar(g_h, acc[:, 5, 0:F], g_recip, None, ALU.mult))
                    nc.vector.tensor_scalar(g_below, g_h, 0.0, None, ALU.min).then_inc(g_below_ready, 1)
                    own(t, nc.vector.tensor_scalar(g_h, g_h, 0.0, -1.0, ALU.max, ALU.add))
                    own(t, nc.vector.tensor_tensor(g_h, g_h, g_x, ALU.add))
                    dve.wait_ge(g_exp_ready, t + 1)
                    own(t, nc.vector.tensor_tensor(g_h, g_h, g_below, ALU.add))
                    own(t, nc.vector.reduce_sum(g_mean, g_h, AX_X))
                    own(t, nc.vector.tensor_scalar(g_mean, g_mean, -1.0 / F, None, ALU.mult))
                    own(t, nc.vector.tensor_scalar(g_dev, g_h, g_mean, None, ALU.add))
                    own(t, nc.vector.tensor_tensor(g_sq, g_dev, g_dev, ALU.mult))
                    nc.vector.reduce_sum(g_var, g_sq, AX_X).then_inc(g_var_ready, 1)
                    dve.wait_ge(g_root_ready, t + 1)
                    own(t, nc.vector.tensor_scalar(g_mean, g_var, 1.0 / F, EPS, ALU.mult, ALU.add))
                    own(t, nc.vector.tensor_tensor(g_rstd, g_root, g_root, ALU.mult))
                    own(t, nc.vector.tensor_tensor(g_rstd, g_rstd, g_mean, ALU.mult))
                    own(t, nc.vector.tensor_scalar(g_rstd, g_rstd, -0.5, 1.5, ALU.mult, ALU.add))
                    own(t, nc.vector.tensor_tensor(g_rstd, g_rstd, g_root, ALU.mult))
                    nc.vector.tensor_scalar(g_dev, g_dev, g_rstd, None, ALU.mult).then_inc(g_out_ready, 1)

            where_needed(dve, general)

        @block.tensor
        def _(pe):
            pe.wait_ge(consts_ready, 1)
            pe.wait_ge(w_loaded, 32)
            for n, (what, g) in enumerate(products):
                bank = acc[:, n % BANKS]
                if n >= BANKS:
                    taken(pe, n - BANKS)
                if what == "wt":
                    last = nc.tensor.transpose(bank[0:F, 0:F], w_in[0:F, :], ident[0:F, 0:F])
                elif what == "wa":
                    taken(pe, number[("wt", 0)])
                    pe.wait_ge(a_loaded, 16)
                    last = nc.tensor.matmul(bank[:, 0:2], wt2.rearrange("f r k -> f (r k)"), a_in[:, :],
                                            start=True, stop=True)
                elif what == "xt":
                    pe.wait_ge(x_loaded, 16)
                    for i in range(4):
                        u = 4 * g + i
                        last = nc.tensor.transpose(bank[:, P * i:P * i + P],
                                                   x_all[:, 2 * u:2 * u + 2].rearrange("p t f -> p (t f)"), ident)
                elif what == "h":
                    taken(pe, number[("xt", g // 2)])
                    taken(pe, number[("wa", 0)])
                    pe.wait_ge(w_placed, 1)
                    for i in range(2):
                        last = nc.tensor.matmul(bank[:, 2 * (F + 2) * i:2 * (F + 2) * (i + 1)], xT[:, 2 * g + i],
                                                wblk.rearrange("p r f -> p (r f)"), start=True, stop=True)
                elif what == "f1":
                    taken(pe, number[("xt", g // 2)])
                    last = nc.tensor.matmul(bank, wa1[:, g % 2],
                                            xT[:, 4 * (g // 2):4 * (g // 2) + 4].rearrange("p u w -> p (u w)"),
                                            start=True, stop=True)
                else:
                    pe.wait_ge(hcol_ready, 1)
                    last = nc.tensor.matmul(bank[:, 0:F1], ones[:], hcol[:], start=True, stop=True)
                last.then_inc(product_made, 1)
            for n in range(len(products) - BANKS, len(products)):
                taken(pe, n)

            def turn(slot, b, place):
                for k in range(T):
                    last = nc.tensor.transpose(turned[:, place, P * k:P * k + P], marks[:, slot, k, P * b:P * b + P],
                                               ident16[:])
                last.then_inc(turned_done, 1)

            def zero(b):
                nc.tensor.matmul(acc[:, b].rearrange("p (o c) -> p o c", c=P), zeros[:],
                                 zeros[:].rearrange("p (o c) -> p o c", o=1).to_broadcast([P, 4, P]), start=True, stop=True)

            for b in range(BANKS):
                zero(b)
            edges_marked(pe, 1)
            turn(0, 0, 0)
            turn(0, 1, 1)

            def pair(s, m, last):
                pe.wait_ge(parts_ready, m + 1)
                for i in range(STEPS):
                    n = s * NB + (m * STEPS + i)
                    pe.wait_ge(neg_made, n + 1)
                    ahead = i + 2
                    if not (last and ahead >= STEPS):
                        if ahead % B == 0:
                            edges_marked(pe, s * CH + (m * 2 + (ahead // B + 1)))
                        turn(ahead // B % 2, ahead % B, i % 2)
                    for kind, edges in enumerate((pos, neg)):
                        weights = parts[:, bass.ds(m * STEPS + i, 1), kind].rearrange("p t c -> p (t c)")
                        for k in range(T):
                            ins = nc.tensor.matmul(at(kind, k), edges[:, i % 4, P * k:P * k + P], weights,
                                                   start=False, stop=True, skip_group_check=True)
                    ins.then_inc(main_done, 1)

            with pe.Fori(0, S - 1) as s:
                with pe.Fori(0, PAIRS) as m:
                    pair(s, m, False)
                for b in range(BANKS):
                    pe.wait_ge(acc_taken, s * BANKS + (b + 1))
                    zero(b)
            with pe.Fori(0, PAIRS - 1) as m:
                pair(S - 1, m, False)
            pair(S - 1, PAIRS - 1, True)

            def general():
                pe.wait_ge(g_ident_ready, 2)
                for g in range(NB // 4):
                    if g >= 4:
                        pe.wait_ge(g_row_taken, g - 3)
                    for i in range(4):
                        last = nc.tensor.matmul(acc[:, g % 4, P * i:P * i + P],
                                                f12[:, 4 * g + i, 1:2].to_broadcast([P, P]), g_ident, start=True, stop=True)
                    last.then_inc(g_row_made, 1)
                pe.wait_ge(g_row_taken, NB // 4)

                def turn_weights(g):
                    for i in range(4):
                        last = nc.tensor.transpose(acc[:, g % 4, P * i:P * i + P],
                                                   g_scores[:, P * (4 * g + i):P * (4 * g + i + 1)], g_ident)
                    last.then_inc(g_turns, 1)

                with pe.Fori(0, NB) as t:
                    pe.wait_ge(g_weighted, t + 1)
                    turn_weights(0)
                    for g in range(NB // 4):
                        if g + 1 < NB // 4:
                            turn_weights(g + 1)
                        pe.wait_ge(g_copied, t * (NB // 4) + (g + 1))
                        for i in range(4):
                            last = nc.tensor.matmul(acc[:, 5, 0:F], g_turned[:, g % 4, P * i:P * i + P],
                                                    h[:, 4 * g + i, 0:F], start=(g == 0 and i == 0),
                                                    stop=(g == NB // 4 - 1 and i == 3))
                    last.then_inc(g_added, 1)

            where_needed(pe, general)


_INS = ["x", "adj", "L0_gnn_W", "L0_gnn_a"]


def kernel(**inputs):
    import numpy as _np
    import concourse.bacc as _bacc
    from concourse import mybir as _mybir
    from concourse.bass_utils import run_bass_kernel_spmd as _run

    nc = _bacc.Bacc("TRN2", target_bir_lowering=False, num_devices=1)
    arrays, args = {}, []
    for name in _INS:
        arr = _np.ascontiguousarray(inputs[name])
        arrays[f"in_{name}_dram"] = arr
        args.append(nc.dram_tensor(f"in_{name}_dram", arr.shape, _mybir.dt.from_np(arr.dtype), kind="ExternalInput").ap())
    out = nc.dram_tensor("out_0_dram", inputs["x"].shape, _mybir.dt.float32, kind="ExternalOutput").ap()
    gat_layer(nc, *args, out)
    return _run(nc, [arrays], core_ids=[0]).results[0]["out_0_dram"]
```

```python
from contextlib import ExitStack

import numpy as np

import concourse.bass as bass
from concourse import mybir

P = 128
ALU = mybir.AluOpType
ACT = mybir.ActivationFunctionType
AX_X = mybir.AxisListType.X
F32, F16, BF16, I32, U32 = mybir.dt.float32, mybir.dt.float16, mybir.dt.bfloat16, mybir.dt.int32, mybir.dt.uint32
RMAX, RADD = bass.bass_isa.ReduceOp.max, bass.bass_isa.ReduceOp.add

SLOPE = 0.01
EPS = 1e-5
ROWS = 1024
T = ROWS // P
COLS = 1024
B = COLS // P
HALF = T // 2
SCALE = 128.0
BY = {"dve": (0, 4), "act": (1, 5, 6), "pool": (2, 3, 7)}


def gat_layer(nc, x, adj, W, a, out):
    N, F = x.shape
    S = N // ROWS
    NB = N // P
    CH = N // COLS
    PAIRS = CH // 2
    F1 = F + 1
    GC = 2 * F1
    PER_BANK = 512 // GC
    SPANS = [(k, min(k + PER_BANK, T)) for k in range(0, T, PER_BANK)]
    AB = len(SPANS)
    STEPS = 2 * B
    assert F == 64 and N % ROWS == 0 and CH % 2 == 0 and 2 * AB + 2 == 8

    x_rows = x.rearrange("(s g p e) f -> s p g (e f)", p=P, g=2, e=HALF)
    out_rows = out.rearrange("(s g p e) f -> s p g (e f)", p=P, g=2, e=HALF)
    adj_halves = adj.rearrange("(s g p e) (c w) -> s c g p e w", p=P, g=2, e=HALF, w=COLS)

    TINY = 2.0 ** -100
    LIMITS = (6.0, 448.0 ** 2, NB * F / 64.0, 2.0 ** 98)

    with ExitStack() as ctx:
        def sb(name, shape, dt):
            return ctx.enter_context(nc.sbuf_tensor(name, shape, dt))

        def sem(name):
            return ctx.enter_context(nc.semaphore(name))

        acc = ctx.enter_context(nc.psum_tensor("acc", [P, 2 * AB, 512], F32))
        turned = ctx.enter_context(nc.psum_tensor("turned", [P, 2, ROWS], BF16))

        ring = sb("ring", [P, 4, HALF, COLS], I32)
        marks = sb("marks", [P, 2, T, COLS], BF16)
        signs = sb("signs", [P, 4, ROWS], BF16)
        edges = sb("edges", [P, 2, 4, ROWS], BF16)
        f1row = sb("f1row", [P, 2, ROWS], F32)
        f1col = sb("f1col", [P, T], F32)
        parts = sb("parts", [P, NB, 2, GC], F16)
        h = sb("h", [P, NB, F1], F32)
        f12 = sb("f12", [P, NB, 2], F32)
        f2tiny = sb("f2tiny", [P, NB], F32)
        a_in = sb("a_in", [F, 2], F32)
        ident16 = sb("ident16", [P, P], BF16)
        zeros = sb("zeros", [P, P], BF16)
        ones = sb("ones", [P, P], F32)
        ab = sb("ab", [P, 2, NB, 1], F32)
        stat = sb("stat", [P, 1], F32)
        bound = sb("bound", [P, 4], F32)
        squares = sb("squares", [P, CH], F32)
        bounds = sb("bounds", [P, 4], F32)
        beyond = sb("beyond", [P, 2], F32)
        flag = sb("flag", [P, 1], I32)
        fmax = sb("fmax", [P, 3], F32)
        hcol = sb("hcol", [P, F1], F32)
        hsum = sb("hsum", [P, 1, F1], F32)
        sums = sb("sums", [P, 2, T, F1], F32)
        xin = sb("xin", [P, T, F], F32)
        dev = sb("dev", [P, T, F], F32)
        tiny = sb("tiny", [P, 6, T, 1], F32)

        pos, neg = edges[:, 0], edges[:, 1]
        x_all = edges[:].rearrange("p k a w -> p (k a w)").bitcast(F32).rearrange("p (g e f) -> p g e f", e=HALF, f=F)
        wt2 = sb("wt2", [F, 2, F], F32)
        wblk = sb("wblk", [P, 2, F + 2], F32)
        w_in = sb("w_in", [P, F], F32)
        ident = sb("ident", [P, P], F32)
        q = sb("q", [P, 2, NB], F32)
        z = sb("z", [P, 2, NB], F32)
        wide = sums
        alone, recip, mean, var, rstd, work = (tiny[:, i] for i in range(6))
        xT = parts[:].rearrange("p t k c -> p (t k c)")[:, 0:NB * F * 2].bitcast(F32)

        x_loaded, w_loaded, a_loaded = sem("x_loaded"), sem("w_loaded"), sem("a_loaded")
        adj_loaded = [sem(f"adj_loaded{i}") for i in range(4)]
        marked = {e: sem(f"marked_{e}") for e in ("dve", "act", "pool")}
        consts_ready, w_placed = sem("consts_ready"), sem("w_placed")
        product_made = sem("product_made")
        product_taken = {"dve": sem("product_taken_dve"), "act": sem("product_taken_act")}
        stat_ready, fmax_ready, shift_ready = sem("stat_ready"), sem("fmax_ready"), sem("shift_ready")
        q_ready, q_scaled, z_ready, ab_ready = sem("q_ready"), sem("q_scaled"), sem("z_ready"), sem("ab_ready")
        parts_ready = {kind: sem(f"parts_ready{kind}") for kind in range(2)}
        f1col_ready, f1row_made, f1row_taken = sem("f1col_ready"), sem("f1row_made"), sem("f1row_taken")
        f2tiny_ready, squares_ready = sem("f2tiny_ready"), sem("squares_ready")
        hcol_ready, hsum_ready = sem("hcol_ready"), sem("hsum_ready")
        turned_done, signs_made = sem("turned_done"), sem("signs_made")
        edges_made, main_done = sem("edges_made"), sem("main_done")
        acc_taken, agg_ready, recip_ready = sem("acc_taken"), sem("agg_ready"), sem("recip_ready")
        xin_loaded, below_ready, exp_ready = sem("xin_loaded"), sem("below_ready"), sem("exp_ready")
        y_ready, var_ready, seed_ready = sem("y_ready"), sem("var_ready"), sem("seed_ready")
        out_ready, dev_free = sem("out_ready"), sem("dev_free")
        last_below, last_exp, last_out = sem("last_below"), sem("last_exp"), sem("last_out")
        bound_ready, bounds_ready, flag_ready = sem("bound_ready"), sem("bounds_ready"), sem("flag_ready")
        g_adj_loaded, g_x_loaded, g_stored, g_row_made, g_row_taken = (
            sem(n) for n in ("g_adj_loaded", "g_x_loaded", "g_stored", "g_row_made", "g_row_taken"))
        g_scored, g_masked, g_weighted, g_turns, g_copied, g_added = (
            sem(n) for n in ("g_scored", "g_masked", "g_weighted", "g_turns", "g_copied", "g_added"))
        g_below_ready, g_exp_ready, g_var_ready, g_root_ready, g_out_ready, g_dve_own, g_act_own = (
            sem(n) for n in ("g_below_ready", "g_exp_ready", "g_var_ready", "g_root_ready", "g_out_ready",
                             "g_dve_own", "g_act_own"))
        dve_own, act_own, pool_own = sem("dve_own"), sem("act_own"), sem("pool_own")
        var_chain, high_taken = sem("var_chain"), sem("high_taken")

        passed = {nc.sync: sem("passed_sync"), nc.scalar: sem("passed_scalar"), nc.vector: sem("passed_vector"),
                  nc.gpsimd: sem("passed_gpsimd"), nc.tensor: sem("passed_tensor")}

        def flat(rows):
            return rows[:].rearrange("p (g e) f -> p g (e f)", e=HALF)

        def hold(eng, signal, value):
            eng.wait_ge(signal, value).then_inc(passed[eng], 1)

        def at(kind, k):
            return acc[:, AB * kind + k // PER_BANK, GC * (k % PER_BANK):GC * (k % PER_BANK + 1)]

        products = [("wt", 0), ("wa", 0)] + [("xt", g) for g in range(NB // 8)] \
            + [("h", g) for g in range(4)] + [("f1", g) for g in range(4)] + [("h", g) for g in range(4, NB // 4)]
        number = {p: n for n, p in enumerate(products)}
        BANKS = 2 * AB

        def taken(eng, n):
            eng.wait_ge(product_taken["act" if n % 2 else "dve"], n // 2 + 1)

        def take_products(eng, engine, copy):
            for n, (what, g) in enumerate(products):
                if ("act" if n % 2 else "dve") != engine:
                    continue
                bank = acc[:, n % BANKS]
                eng.wait_ge(product_made, n + 1)
                if what == "wt":
                    copy(wt2[:, 0], bank[0:F, 0:F])
                    last = copy(wt2[:, 1], bank[0:F, 0:F])
                elif what == "wa":
                    for r in range(2):
                        rows = slice(F * r, F * r + F)
                        last = copy(wblk[rows, r, F:F + 2], bank[rows, 0:2])
                elif what == "xt":
                    last = copy(xT[:, 4 * P * g:4 * P * (g + 1)], bank)
                elif what == "h":
                    rows = bank[:, 0:4 * (F + 2)].rearrange("p (t f) -> p t f", f=F + 2)
                    copy(h[:, 4 * g:4 * g + 4, 0:F], rows[:, :, 0:F])
                    last = copy(f12[:, 4 * g:4 * g + 4, :], rows[:, :, F:F + 2])
                else:
                    last = copy(f1row[:, g // 2, 512 * (g % 2):512 * (g % 2 + 1)], bank)
                last.then_inc(product_taken[engine], 1)
                yield what, g

        def edges_marked(eng, chunks, tiles=0):
            for name, ks in BY.items():
                count = chunks * len(ks) + sum(k < tiles for k in ks)
                if not (isinstance(count, int) and count == 0):
                    hold(eng, marked[name], count)

        def may_mark(eng, s, c, k):
            hold(eng, adj_loaded[2 * (c % 2) + k // HALF], (s * CH + c - c % 2) * 8 + 16)
            if not (isinstance(s, int) and s == 0 and c < 2):
                hold(eng, turned_done, (s * CH + c - 1) * B)

        def tile_of(c, k):
            return ring[:, 2 * (c % 2) + k // HALF, k % HALF], marks[:, c % 2, k]

        def columns(b):
            first = P * HALF * (b // HALF) + b % HALF
            return slice(first, first + HALF * (P - 1) + 1, HALF)

        def over_supers(eng, one):
            one(0, True, False)
            with eng.Fori(1, S - 1) as s:
                one(s, False, False)
            one(S - 1, False, True)

        def weigh(e, link, kind, c):
            blocks = slice(B * c, B * c + B)
            w = q[:, kind, blocks].rearrange("p (t o) -> p t o", o=1).to_broadcast([P, B, F1])
            high, low = parts[:, blocks, kind, 0:F1], parts[:, blocks, kind, F1:GC]
            link(e.tensor_tensor(wide[:, kind], h[:, blocks], w, ALU.mult))
            link(e.tensor_copy(high, wide[:, kind]))
            return e.tensor_tensor(low, wide[:, kind], high, ALU.subtract)

        def aggregate(e, link, s):
            for kind in range(2):
                last = e.tensor_tensor(sums[:, kind], sums[:, kind],
                                       ab[:, kind, bass.ds(s * T, T)].to_broadcast([P, T, F1]), ALU.mult)
            link(last)
            link(e.tensor_tensor(sums[:, 0], sums[:, 0], sums[:, 1], ALU.add))
            link(e.tensor_scalar(alone, sums[:, 0, :, F:F1], 0.0, None, ALU.is_le))
            link(e.tensor_tensor(sums[:, 1], hsum[:].to_broadcast([P, T, F1]), alone.to_broadcast([P, T, F1]), ALU.mult))
            return e.tensor_tensor(sums[:, 0], sums[:, 0], sums[:, 1], ALU.add)

        def average(e, link):
            link(e.tensor_tensor(num, num, recip.to_broadcast([P, T, F]), ALU.mult))
            return e.tensor_scalar(below, num, 0.0, None, ALU.min)

        def above(e, link):
            link(e.tensor_scalar(num, num, 0.0, -1.0, ALU.max, ALU.add))
            link(e.tensor_tensor(xin[:], xin[:], num, ALU.add))

        def spread(link):
            link(nc.vector.tensor_reduce(mean, xin[:], AX_X, ALU.add))
            link(nc.vector.tensor_scalar(mean, mean, -1.0 / F, None, ALU.mult))
            link(nc.vector.tensor_tensor(dev[:], xin[:], mean.to_broadcast([P, T, F]), ALU.add))
            link(nc.vector.tensor_tensor(below, dev[:], dev[:], ALU.mult))
            link(nc.vector.tensor_reduce(var, below, AX_X, ALU.add))
            return seed(link, var, rstd)

        def seed(link, v, r):
            link(nc.vector.tensor_scalar(v, v, 1.0 / F, EPS, ALU.mult, ALU.add))
            link(nc.vector.tensor_scalar(r.bitcast(I32), v.bitcast(I32), 1, None, ALU.logical_shift_right))
            return nc.vector.tensor_scalar(r.bitcast(I32), r.bitcast(I32), -1.0, float(0x5F3759DF), ALU.mult, ALU.add)

        def newton(e, link, v, r, t):
            for _ in range(3):
                link(e.tensor_tensor(t, r, r, ALU.mult))
                link(e.tensor_tensor(t, t, v, ALU.mult))
                link(e.tensor_scalar(t, t, -0.5, 1.5, ALU.mult, ALU.add))
                link(e.tensor_tensor(r, r, t, ALU.mult))

        def normed(e):
            return e.tensor_tensor(dev[:], dev[:], rstd.to_broadcast([P, T, F]), ALU.mult)

        halves = ring[:].rearrange("p (a b) t w -> p a (b t w)", a=2)
        g_adj, g_scores = halves[:, 0], halves[:, 1].bitcast(F32)
        g_f2row = marks[:].rearrange("p a t w -> p (a t w)").bitcast(F32)
        g_mask = pos.rearrange("p a w -> p (a w)").bitcast(F32)
        g_turned = neg.rearrange("p a w -> p (a w)").bitcast(F32).rearrange("p (g w) -> p g w", g=4)
        g_h, g_below, g_sq, g_dev, g_x = sums[:, 0, 0, 0:F], sums[:, 0, 1, 0:F], sums[:, 0, 2, 0:F], dev[:, 0], xin[:, 0]
        g_max, g_sum, g_recip, g_mean, g_var, g_root, g_rstd = (sums[:, 1, i, 0:1] for i in range(7))

        num, below = sums[:, 0, :, 0:F], sums[:, 1, :, 0:F]

        def where_needed(eng, general):
            eng.wait_ge(flag_ready, 1)
            with eng.If(eng.value_load(flag[0:1, 0:1], min_val=0, max_val=1) > 0):
                general()

        block = ctx.enter_context(nc.Block())

        @block.sync
        def _(sp):
            def load(s, c):
                for half in range(2):
                    edges_marked(sp, s * CH + c - 2, (half + 1) * HALF)
                    src = adj_halves[bass.ds(s, 1), c, half].rearrange("s p e w -> p (s e) w")
                    sp.dma_start(ring[:, 2 * (c % 2) + half], src).then_inc(adj_loaded[2 * (c % 2) + half], 16)

            def rows_in(s):
                if not (isinstance(s, int) and s == 0):
                    hold(sp, out_ready, s)
                sp.dma_start(flat(xin), x_rows[bass.ds(s, 1)].rearrange("s p g w -> p (s g) w")).then_inc(xin_loaded, 16)

            sp.dma_start(w_in[0:F, :], W).then_inc(w_loaded, 16)
            sp.dma_start(w_in[F:2 * F, :], W).then_inc(w_loaded, 16)
            with nc.allow_non_contiguous_dma(reason="128 numbers"):
                sp.dma_start(a_in[:, :], a.rearrange("(c f) o -> f (c o)", c=2)).then_inc(a_loaded, 16)
            sp.dma_start(x_all.rearrange("p g e f -> p g (e f)"), x.rearrange("(g p e) f -> p g (e f)", p=P, e=HALF)) \
                .then_inc(x_loaded, 16)
            for c in range(2):
                for half in range(2):
                    sp.dma_start(ring[:, 2 * c + half], adj_halves[0, c, half]).then_inc(adj_loaded[2 * c + half], 16)

            def one(s, first, last):
                for c in range(CH):
                    if not first or c > 1:
                        load(s, c)
                    if c == 1 and not first:
                        rows_in(s - 1)

            over_supers(sp, one)
            rows_in(S - 1)
            sp.wait_ge(last_out, 1)
            sp.dma_start(out_rows[S - 1], flat(dev)).then_inc(dev_free, 16)
            sp.wait_ge(dev_free, 16 * (S + 1))

            def general():
                rows_of = [v.rearrange("(g p e) c -> g p e c", p=P, e=HALF) for v in (adj, x, out)]
                with sp.Fori(0, NB // HALF) as g:
                    with sp.Fori(0, HALF) as e:
                        t = g * HALF + e
                        adj_rows, x_rows, out_rows = (
                            v[bass.ds(g, 1), :, bass.ds(e, 1)].rearrange("g p e c -> p (g e c)") for v in rows_of)
                        sp.dma_start(g_adj, adj_rows).then_inc(g_adj_loaded, 16)
                        sp.dma_start(g_x, x_rows).then_inc(g_x_loaded, 16)
                        hold(sp, g_out_ready, t + 1)
                        sp.dma_start(out_rows, g_dev).then_inc(g_stored, 16)
                        hold(sp, g_stored, t * 16 + 16)

            where_needed(sp, general)

        @block.gpsimd
        def _(pool):
            nc.gpsimd.memset(ident[:], 0.0).then_inc(pool_own, 1)
            pool.wait_ge(pool_own, 1)
            nc.gpsimd.affine_select(out=ident[:], in_=ident[:], compare_op=ALU.not_equal, fill=1.0, base=0,
                                    pattern=[[-1, P]], channel_multiplier=1).then_inc(pool_own, 1)
            pool.wait_ge(pool_own, 2)
            nc.gpsimd.tensor_copy(ident16[:], ident[:])
            nc.gpsimd.memset(wblk[:], 0.0)
            nc.gpsimd.memset(ones[:], 1.0)
            nc.gpsimd.memset(zeros[:].bitcast(F32), 0.0)
            nc.gpsimd.memset(h[:, :, F:F1], 1.0).then_inc(consts_ready, 1)

            def mark(s, c, tiles=BY["pool"]):
                for k in tiles:
                    may_mark(pool, s, c, k)
                    src, dst = tile_of(c, k)
                    nc.gpsimd.tensor_scalar(dst, src, 0, None, ALU.is_le).then_inc(marked["pool"], 1)

            def static_link(ins):
                own[0] += 1
                ins.then_inc(pool_own, 1)
                pool.wait_ge(pool_own, own[0])

            own = [2]
            mark(0, 0)
            mark(0, 1, BY["pool"][:2])
            pool.wait_ge(stat_ready, 1)
            nc.gpsimd.partition_all_reduce(fmax[:, 0:1], stat[:], P, RMAX).then_inc(fmax_ready, 1)
            pool.wait_ge(q_scaled, 1)
            pool.wait_ge(product_made, len(products))
            weigh(nc.gpsimd, static_link, 1, 0).then_inc(parts_ready[1], 1)
            mark(0, 1, BY["pool"][2:])

            LINKS = 4 + 1 + 2 + 12

            def one(s, first, last):
                count = [0]

                def link(ins):
                    count[0] += 1
                    ins.then_inc(pool_own, 1)
                    hold(pool, pool_own, (s - 1) * LINKS + (own[0] + count[0]))

                for c in range(CH):
                    if first and c + 1 < CH:
                        pool.wait_ge(parts_ready[1], c + 1)
                        weigh(nc.gpsimd, static_link, 1, c + 1).then_inc(parts_ready[1], 1)
                    if not (last and c == CH - 1) and not (first and c == 0):
                        mark(s + (c + 1) // CH, (c + 1) % CH)
                    if first and c == 5:
                        pool.wait_ge(hcol_ready, 1)
                        nc.gpsimd.partition_all_reduce(hsum[:, 0], hcol[:], P, RADD).then_inc(hsum_ready, 1)
                    if first:
                        continue
                    if c == 0:
                        hold(pool, acc_taken, s * BANKS)
                        pool.wait_ge(ab_ready, 1)
                        pool.wait_ge(hsum_ready, 1)
                        aggregate(nc.gpsimd, link, s - 1).then_inc(agg_ready, 1)
                    if c == 2:
                        hold(pool, recip_ready, s)
                        average(nc.gpsimd, link).then_inc(below_ready, 1)
                        hold(pool, xin_loaded, s * 16)
                        above(nc.gpsimd, link)
                    if c == 4:
                        hold(pool, exp_ready, s)
                        nc.gpsimd.tensor_tensor(xin[:], xin[:], below, ALU.add).then_inc(y_ready, 1)
                    if c == 5:
                        hold(pool, seed_ready, s)
                        newton(nc.gpsimd, link, var, rstd, work)
                        normed(nc.gpsimd).then_inc(out_ready, 1)
                assert first or count[0] == LINKS

            over_supers(pool, one)
            pool.wait_ge(bound_ready, 2)
            nc.gpsimd.partition_all_reduce(bounds[:], bound[:], P, RMAX).then_inc(bounds_ready, 1)

        @block.scalar
        def _(act):
            def copy(dst, src):
                return nc.scalar.copy(dst, src)

            act.wait_ge(consts_ready, 1)
            act.wait_ge(w_loaded, 32)
            for r in range(2):
                rows = slice(F * r, F * r + F)
                last = copy(wblk[rows, r, 0:F], w_in[rows, :])
            last.then_inc(w_placed, 1)
            def mark(s, c, k):
                may_mark(act, s, c, k)
                src, dst = tile_of(c, k)
                nc.scalar.activation(dst, src, ACT.Relu, bias=ones[:, 0:1], scale=-1.0).then_inc(marked["act"], 1)

            early = {("h", 1): (0, 1), ("h", 5): (0, 5), ("h", 7): (0, 6), ("h", 11): (1, 1)}
            for product in take_products(act, "act", copy):
                if product in early:
                    mark(0, *early[product])
            act.wait_ge(shift_ready, 1)
            nc.scalar.activation(q[:, 0], f12[:, :, 1], ACT.Exp, bias=fmax[:, 1:2])
            nc.scalar.activation(q[:, 1], f12[:, :, 1], ACT.Exp, bias=fmax[:, 2:3], scale=SLOPE).then_inc(q_ready, 1)
            act.wait_ge(z_ready, 1)
            nc.scalar.activation(ab[:, :, :, 0], z[:], ACT.Exp).then_inc(ab_ready, 1)
            mark(0, 1, 5)
            mark(0, 1, 6)

            act.wait_ge(f2tiny_ready, 1)
            for g in range(4):
                taken(act, number["f1", g])

            def sign(s, jb):
                n = s * NB + jb
                if not (isinstance(s, int) and s == 0 and jb < 4):
                    hold(act, edges_made, n * 2 - 6)
                row = f1row[:, bass.ds(s % 2, 1)].rearrange("p s w -> p (s w)")
                nc.scalar.activation(signs[:, jb % 4], row, ACT.Relu, bias=f2tiny[:, jb:jb + 1], scale=TINY) \
                    .then_inc(signs_made, 1)

            def next_f1(s):
                nc.scalar.copy(f1col[:], f12[:, bass.ds((s + 2) % S * T, T), 0:1].rearrange("p t o -> p (t o)")) \
                    .then_inc(f1col_ready, 1)

            def take_f1(s):
                for b in range(2):
                    hold(act, f1row_made, (s - 1) * 2 + b + 1)
                    nc.scalar.copy(f1row[:, bass.ds((s + 1) % 2, 1), 512 * b:512 * (b + 1)].rearrange("p s w -> p (s w)"),
                                   acc[:, b]).then_inc(f1row_taken, 1)

            def exp_below(s):
                act.wait_ge(below_ready, s + 1)
                nc.scalar.activation(below, below, ACT.Exp).then_inc(exp_ready, 1)

            def rows_out(s):
                hold(act, out_ready, s + 1)
                act.dma_start(out_rows[bass.ds(s, 1)].rearrange("s p g w -> p (s g) w"), flat(dev)).then_inc(dev_free, 16)

            ACT_AT = [1, 3, 5, 7][:len(BY["act"])]

            def one(s, first, last):
                for c in range(CH):
                    if first:
                        if c:
                            act.wait_ge(squares_ready, c)
                        nc.scalar.activation(dev[:], h[:, B * c:B * c + B, 0:F], ACT.Square,
                                             accum_out=squares[:, c:c + 1]).then_inc(squares_ready, 1)
                    if c == 5 and not last:
                        next_f1(s)
                    for i in range(B):
                        sign(s, c * B + i)
                        if i == 3 and c == 0 and not first:
                            take_f1(s)
                        if i in ACT_AT and not (last and c == CH - 1) and not (first and c == 0):
                            mark(s + (c + 1) // CH, (c + 1) % CH, BY["act"][ACT_AT.index(i)])
                    if c == CH - 1 and first:
                        act.wait_ge(squares_ready, CH).then_inc(dev_free, 16)
                    if c == 3 and not first:
                        exp_below(s - 1)
                    if c == 6 and not first:
                        rows_out(s - 1)

            over_supers(act, one)
            act.wait_ge(last_below, 1)
            nc.scalar.activation(below, below, ACT.Exp).then_inc(last_exp, 1)

            def general():
                act.wait_ge(g_row_taken, NB // 4)
                with act.Fori(0, NB) as t:
                    hold(act, g_adj_loaded, t * 16 + 16)
                    nc.scalar.activation(g_scores, g_f2row, ACT.Identity, bias=f12[:, bass.ds(t, 1), 0:1]
                                         .rearrange("p t o -> p (t o)")).then_inc(g_scored, 1)
                    hold(act, g_masked, t + 1)
                    nc.scalar.activation(g_scores, g_scores, ACT.Exp, bias=g_max, accum_out=g_sum).then_inc(g_weighted, 1)
                    hold(act, g_below_ready, t + 1)
                    nc.scalar.activation(g_below, g_below, ACT.Exp).then_inc(g_exp_ready, 1)

            where_needed(act, general)

        @block.vector
        def _(dve):
            own = [0]

            def link(ins):
                own[0] += 1
                ins.then_inc(dve_own, 1)
                dve.wait_ge(dve_own, own[0])

            def copy(dst, src):
                return nc.vector.tensor_copy(dst, src)

            def mark(s, c, k):
                may_mark(dve, s, c, k)
                src, dst = tile_of(c, k)
                nc.vector.tensor_scalar(dst, src, 0, None, ALU.is_le).then_inc(marked["dve"], 1)

            early = {("h", 4): (0, 0), ("h", 8): (0, 4), ("h", 12): (1, 0)}
            for product in take_products(dve, "dve", copy):
                if product in early:
                    mark(0, *early[product])
                if product == ("h", NB // 4 - 2):
                    for g in (NB // 4 - 2, NB // 4 - 1):
                        taken(dve, number[("h", g)])
                    nc.vector.reduce_max(stat[:], f12[:, :, 1], AX_X).then_inc(stat_ready, 1)
                    nc.vector.tensor_scalar(f2tiny[:], f12[:, :, 1], TINY, None, ALU.mult).then_inc(f2tiny_ready, 1)
                    nc.vector.reduce_max(bound[:, 3:4], f12[:, :, 0], AX_X)
                    nc.vector.tensor_reduce(bound[:, 1:2], f12[:, :, 1], AX_X, ALU.min)
                    dve.wait_ge(stat_ready, 1)
                    link(nc.vector.tensor_copy(bound[:, 0:1], stat[:]))
                    nc.vector.tensor_scalar(bound[:, 1:2], bound[:, 1:2], -1.0, None, ALU.mult).then_inc(bound_ready, 1)
            dve.wait_ge(fmax_ready, 1)
            nc.vector.tensor_scalar(fmax[:, 1:2], fmax[:, 0:1], -1.0, None, ALU.mult)
            nc.vector.tensor_scalar(fmax[:, 2:3], fmax[:, 0:1], -SLOPE, None, ALU.mult).then_inc(shift_ready, 1)
            link(nc.vector.tensor_scalar(z[:, 0], f12[:, :, 0], fmax[:, 0:1], 1.0 - SLOPE, ALU.add, ALU.mult))
            link(nc.vector.tensor_scalar(z[:, 1], z[:, 0], -1.0, 0.0, ALU.mult, ALU.min))
            nc.vector.tensor_scalar(z[:, 0], z[:, 0], 0.0, None, ALU.min).then_inc(z_ready, 1)
            dve.wait_ge(q_ready, 1)
            nc.vector.tensor_scalar(q[:], q[:], SCALE, None, ALU.mult).then_inc(q_scaled, 1)
            dve.wait_ge(q_scaled, 1)
            dve.wait_ge(product_made, len(products))
            weigh(nc.vector, link, 0, 0).then_inc(parts_ready[0], 1)
            mark(0, 1, 4)

            def step(s, jb):
                n = s * NB + jb
                dve.wait_ge(turned_done, n + 1)
                dve.wait_ge(signs_made, n + 1)
                if not (isinstance(s, int) and s == 0 and jb < 4):
                    dve.wait_ge(main_done, n - 3)
                nc.vector.tensor_tensor(pos[:, jb % 4], signs[:, jb % 4], turned[:, jb % 2], ALU.is_gt) \
                    .then_inc(edges_made, 1)
                nc.vector.tensor_tensor(neg[:, jb % 4], signs[:, jb % 4], turned[:, jb % 2], ALU.is_equal) \
                    .then_inc(edges_made, 1)

            def take_sums(s):
                dve.wait_ge(main_done, s * NB + NB)
                banks = [(kind, b, k0, k1) for kind in range(2) for b, (k0, k1) in enumerate(SPANS)]
                for i in range(BANKS + 1):
                    if i < BANKS:
                        kind, b, k0, k1 = banks[i]
                        high = acc[:, i, 0:GC * (k1 - k0)].rearrange("p (k c) -> p k c", c=GC)[:, :, 0:F1]
                        copy(sums[:, kind, k0:k1], high).then_inc(high_taken, 1)
                    if i:
                        kind, b, k0, k1 = banks[i - 1]
                        low = acc[:, i - 1, 0:GC * (k1 - k0)].rearrange("p (k c) -> p k c", c=GC)[:, :, F1:GC]
                        dve.wait_ge(high_taken, s * BANKS + i)
                        nc.vector.tensor_tensor(sums[:, kind, k0:k1], sums[:, kind, k0:k1], low, ALU.add) \
                            .then_inc(acc_taken, 1)

            def reciprocal(s):
                dve.wait_ge(agg_ready, s + 1)
                nc.vector.reciprocal(recip, sums[:, 0, :, F:F1]).then_inc(recip_ready, 1)

            def linked(chain, value, ins):
                ins.then_inc(chain, 1)
                dve.wait_ge(chain, value)

            DVE_AT = [2, 5]

            def one(s, first, last):
                for c in range(CH):
                    if first and c + 1 < CH:
                        dve.wait_ge(parts_ready[0], c + 1)
                        weigh(nc.vector, link, 0, c + 1).then_inc(parts_ready[0], 1)
                    for i in range(B):
                        step(s, c * B + i)
                        if c == 0 and i == 1 and not first:
                            take_sums(s - 1)
                        if i in DVE_AT and not (last and c == CH - 1) and not (first and c == 0):
                            mark(s + (c + 1) // CH, (c + 1) % CH, BY["dve"][DVE_AT.index(i)])
                    if c == CH - 1 and first:
                        dve.wait_ge(squares_ready, CH)
                        nc.vector.reduce_sum(bound[:, 2:3], squares[:], AX_X).then_inc(bound_ready, 1)
                    if c == 4 and first:
                        nc.vector.tensor_reduce(hcol[:], h[:].rearrange("p t f -> p f t"), AX_X, ALU.add) \
                            .then_inc(hcol_ready, 1)
                    if c == 1 and not first:
                        reciprocal(s - 1)
                    if c == 4 and not first:
                        count = [0]

                        def in_loop(ins):
                            count[0] += 1
                            linked(var_chain, (s - 1) * 7 + count[0], ins)

                        dve.wait_ge(y_ready, s)
                        dve.wait_ge(dev_free, s * 16)
                        spread(in_loop).then_inc(seed_ready, 1)
                        assert count[0] == 7

            over_supers(dve, one)
            take_sums(S - 1)
            dve.wait_ge(acc_taken, S * BANKS)
            dve.wait_ge(hsum_ready, 1)
            dve.wait_ge(ab_ready, 1)
            link(aggregate(nc.vector, link, S - 1))
            link(nc.vector.reciprocal(recip, sums[:, 0, :, F:F1]))
            average(nc.vector, link).then_inc(last_below, 1)
            dve.wait_ge(xin_loaded, S * 16)
            above(nc.vector, link)
            dve.wait_ge(last_exp, 1)
            link(nc.vector.tensor_tensor(xin[:], xin[:], below, ALU.add))
            dve.wait_ge(dev_free, S * 16)
            link(spread(link))
            newton(nc.vector, link, var, rstd, work)
            normed(nc.vector).then_inc(last_out, 1)
            dve.wait_ge(bounds_ready, 1)
            link(nc.vector.tensor_tensor(beyond[:, 0:1], bounds[:, 0:1], bounds[:, 1:2], ALU.add))
            link(nc.vector.tensor_scalar(beyond[:, 0:1], beyond[:, 0:1], LIMITS[0], None, ALU.is_le))
            link(nc.vector.tensor_scalar(beyond[:, 1:2], bounds[:, 2:3], LIMITS[1], None, ALU.is_le))
            link(nc.vector.tensor_tensor(beyond[:, 0:1], beyond[:, 0:1], beyond[:, 1:2], ALU.mult))
            link(nc.vector.tensor_scalar(beyond[:, 1:2], bounds[:, 2:3], LIMITS[2], None, ALU.is_ge))
            link(nc.vector.tensor_tensor(beyond[:, 0:1], beyond[:, 0:1], beyond[:, 1:2], ALU.mult))
            link(nc.vector.tensor_tensor(beyond[:, 1:2], bounds[:, 0:1], bounds[:, 3:4], ALU.max))
            link(nc.vector.tensor_scalar(beyond[:, 1:2], beyond[:, 1:2], LIMITS[3], None, ALU.is_le))
            link(nc.vector.tensor_tensor(beyond[:, 0:1], beyond[:, 0:1], beyond[:, 1:2], ALU.mult))
            nc.vector.tensor_scalar(flag[:], beyond[:, 0:1], 0.0, None, ALU.is_equal).then_inc(flag_ready, 1)
            def general():
                links = [0]

                def own(t, ins):
                    links[0] += 1
                    ins.then_inc(g_dve_own, 1)
                    dve.wait_ge(g_dve_own, t * OWN + links[0])

                for g in range(NB // 4):
                    dve.wait_ge(g_row_made, g + 1)
                    copy(g_f2row[:, 4 * P * g:4 * P * (g + 1)].rearrange("p (w e) -> p e w", e=HALF),
                         acc[:, g % 4].rearrange("p (e w) -> p e w", e=HALF)).then_inc(g_row_taken, 1)

                QUARTER = N // 4
                OWN = 3 * 4 + 11 + 3 + 12
                with dve.Fori(0, NB) as t:
                    dve.wait_ge(g_adj_loaded, t * 16 + 16)
                    dve.wait_ge(g_x_loaded, t * 16 + 16)
                    dve.wait_ge(g_scored, t + 1)
                    for i in range(4):
                        span = slice(QUARTER * i, QUARTER * (i + 1))
                        own(t, nc.vector.scalar_tensor_tensor(g_scores[:, span], g_scores[:, span], SLOPE,
                                                                      g_scores[:, span], ALU.mult, ALU.max))
                        nc.vector.scalar_tensor_tensor(g_scores[:, span], g_adj[:, span], 0.0, g_scores[:, span],
                                                       ALU.is_gt, ALU.mult)
                        own(t, nc.vector.tensor_scalar(g_mask, g_adj[:, span], 0.0, -1e12, ALU.is_le, ALU.mult))
                        own(t, nc.vector.tensor_tensor(g_scores[:, span], g_scores[:, span], g_mask, ALU.add))
                    own(t, nc.vector.reduce_max(g_max, g_scores, AX_X))
                    nc.vector.tensor_scalar(g_max, g_max, -1.0, None, ALU.mult).then_inc(g_masked, 1)
                    for g in range(NB // 4):
                        dve.wait_ge(g_turns, t * (NB // 4) + (g + 1))
                        copy(g_turned[:, g % 4], acc[:, g % 4]).then_inc(g_copied, 1)
                    dve.wait_ge(g_added, t + 1)
                    own(t, nc.vector.reciprocal(g_recip, g_sum))
                    own(t, nc.vector.tensor_scalar(g_h, acc[:, 5, 0:F], g_recip, None, ALU.mult))
                    nc.vector.tensor_scalar(g_below, g_h, 0.0, None, ALU.min).then_inc(g_below_ready, 1)
                    own(t, nc.vector.tensor_scalar(g_h, g_h, 0.0, -1.0, ALU.max, ALU.add))
                    own(t, nc.vector.tensor_tensor(g_h, g_h, g_x, ALU.add))
                    dve.wait_ge(g_exp_ready, t + 1)
                    own(t, nc.vector.tensor_tensor(g_h, g_h, g_below, ALU.add))
                    own(t, nc.vector.reduce_sum(g_mean, g_h, AX_X))
                    own(t, nc.vector.tensor_scalar(g_mean, g_mean, -1.0 / F, None, ALU.mult))
                    own(t, nc.vector.tensor_scalar(g_dev, g_h, g_mean, None, ALU.add))
                    own(t, nc.vector.tensor_tensor(g_sq, g_dev, g_dev, ALU.mult))
                    own(t, nc.vector.reduce_sum(g_var, g_sq, AX_X))
                    own(t, seed(lambda ins: own(t, ins), g_var, g_rstd))
                    newton(nc.vector, lambda ins: own(t, ins), g_var, g_rstd, g_mean)
                    nc.vector.tensor_scalar(g_dev, g_dev, g_rstd, None, ALU.mult).then_inc(g_out_ready, 1)
                assert links[0] == OWN

            where_needed(dve, general)

        @block.tensor
        def _(pe):
            def spread_f1(b, col):
                for i in range(4):
                    last = nc.tensor.matmul(acc[:, b, P * i:P * i + P], col[:, i:i + 1].to_broadcast([P, P]), ident[:],
                                            start=True, stop=True)
                return last

            pe.wait_ge(consts_ready, 1)
            pe.wait_ge(w_loaded, 32)
            for n, (what, g) in enumerate(products):
                bank = acc[:, n % BANKS]
                if n >= BANKS:
                    taken(pe, n - BANKS)
                if what == "wt":
                    last = nc.tensor.transpose(bank[0:F, 0:F], w_in[0:F, :], ident[0:F, 0:F])
                elif what == "wa":
                    taken(pe, number[("wt", 0)])
                    pe.wait_ge(a_loaded, 16)
                    last = nc.tensor.matmul(bank[:, 0:2], wt2[:].rearrange("f r k -> f (r k)"), a_in[:, :],
                                            start=True, stop=True)
                elif what == "xt":
                    pe.wait_ge(x_loaded, 16)
                    for i in range(4):
                        u = 4 * g + i
                        last = nc.tensor.transpose(bank[:, P * i:P * i + P],
                                                   x_all[:, u // 2, 2 * (u % 2):2 * (u % 2) + 2].rearrange("p e f -> p (e f)"), ident[:])
                elif what == "h":
                    taken(pe, number[("xt", g // 2)])
                    taken(pe, number[("wa", 0)])
                    pe.wait_ge(w_placed, 1)
                    for i in range(2):
                        last = nc.tensor.matmul(bank[:, 2 * (F + 2) * i:2 * (F + 2) * (i + 1)], xT[:, P * (2 * g + i):P * (2 * g + i + 1)],
                                                wblk[:].rearrange("p r f -> p (r f)"), start=True, stop=True)
                else:
                    taken(pe, number[("h", g)])
                    last = spread_f1(n % BANKS, f12[:, 4 * g:4 * g + 4, 0:1].rearrange("p t o -> p (t o)"))
                last.then_inc(product_made, 1)
            for n in range(len(products) - BANKS, len(products)):
                taken(pe, n)

            def turn(slot, b, place):
                for k in range(T):
                    last = nc.tensor.transpose(turned[:, place, P * k:P * k + P], marks[:, slot, k, columns(b)],
                                               ident16[:])
                last.then_inc(turned_done, 1)

            def zero(b):
                nc.tensor.matmul(acc[:, b].rearrange("p (o c) -> p o c", c=P), zeros[:],
                                 zeros[:].rearrange("p (o c) -> p o c", o=1).to_broadcast([P, 4, P]), start=True, stop=True)

            for b in range(BANKS):
                zero(b)
            edges_marked(pe, 1)
            turn(0, 0, 0)
            turn(0, 1, 1)

            def pair(s, m, last):
                for i in range(STEPS):
                    if i % B == 0:
                        for kind in range(2):
                            pe.wait_ge(parts_ready[kind], m * 2 + (i // B + 1))
                    n = s * NB + (m * STEPS + i)
                    pe.wait_ge(edges_made, n * 2 + 2)
                    ahead = i + 2
                    if not (last and ahead >= STEPS):
                        if ahead % B == 0:
                            edges_marked(pe, s * CH + (m * 2 + (ahead // B + 1)))
                        turn(ahead // B % 2, ahead % B, i % 2)
                    for kind, edges in enumerate((pos, neg)):
                        weights = parts[:, bass.ds(m * STEPS + i, 1), kind].rearrange("p t c -> p (t c)")
                        for k in range(T):
                            ins = nc.tensor.matmul(at(kind, k), edges[:, i % 4, P * k:P * k + P], weights,
                                                   start=False, stop=True, skip_group_check=True)
                    ins.then_inc(main_done, 1)

            with pe.Fori(0, S - 1) as s:
                with pe.Fori(0, PAIRS) as m:
                    pair(s, m, False)
                pe.wait_ge(f1col_ready, s + 1)
                for b in range(BANKS):
                    pe.wait_ge(acc_taken, s * BANKS + (b + 1))
                    if b < 2:
                        spread_f1(b, f1col[:, 4 * b:4 * b + 4]).then_inc(f1row_made, 1)
                    else:
                        zero(b)
                for b in range(2):
                    pe.wait_ge(f1row_taken, s * 2 + (b + 1))
                    zero(b)
            with pe.Fori(0, PAIRS - 1) as m:
                pair(S - 1, m, False)
            pair(S - 1, PAIRS - 1, True)

            def general():
                for g in range(NB // 4):
                    if g >= 4:
                        pe.wait_ge(g_row_taken, g - 3)
                    for i in range(4):
                        last = nc.tensor.matmul(acc[:, g % 4, P * i:P * i + P],
                                                f12[:, 4 * g + i, 1:2].to_broadcast([P, P]), ident[:], start=True, stop=True)
                    last.then_inc(g_row_made, 1)
                pe.wait_ge(g_row_taken, NB // 4)

                def turn_weights(g):
                    for i in range(4):
                        last = nc.tensor.transpose(acc[:, g % 4, P * i:P * i + P],
                                                   g_scores[:, columns(4 * g + i)], ident[:])
                    last.then_inc(g_turns, 1)

                with pe.Fori(0, NB) as t:
                    pe.wait_ge(g_weighted, t + 1)
                    turn_weights(0)
                    for g in range(NB // 4):
                        if g + 1 < NB // 4:
                            turn_weights(g + 1)
                        pe.wait_ge(g_copied, t * (NB // 4) + (g + 1))
                        for i in range(4):
                            last = nc.tensor.matmul(acc[:, 5, 0:F], g_turned[:, g % 4, P * i:P * i + P],
                                                    h[:, 4 * g + i, 0:F], start=(g == 0 and i == 0),
                                                    stop=(g == NB // 4 - 1 and i == 3))
                    last.then_inc(g_added, 1)

            where_needed(pe, general)


_INS = ["x", "adj", "L0_gnn_W", "L0_gnn_a"]


def kernel(**inputs):
    import numpy as _np
    import concourse.bacc as _bacc
    from concourse import mybir as _mybir
    from concourse.bass_utils import run_bass_kernel_spmd as _run

    nc = _bacc.Bacc("TRN2", target_bir_lowering=False, num_devices=1)
    arrays, args = {}, []
    for name in _INS:
        arr = _np.ascontiguousarray(inputs[name])
        arrays[f"in_{name}_dram"] = arr
        args.append(nc.dram_tensor(f"in_{name}_dram", arr.shape, _mybir.dt.from_np(arr.dtype), kind="ExternalInput").ap())
    out = nc.dram_tensor("out_0_dram", inputs["x"].shape, _mybir.dt.float32, kind="ExternalOutput").ap()
    gat_layer(nc, *args, out)
    return _run(nc, [arrays], core_ids=[0]).results[0]["out_0_dram"]
```

```python
from contextlib import ExitStack

import numpy as np

import concourse.bass as bass
from concourse import mybir

P = 128
ALU = mybir.AluOpType
ACT = mybir.ActivationFunctionType
AX_X = mybir.AxisListType.X
F32, F16, BF16, I32, U32 = mybir.dt.float32, mybir.dt.float16, mybir.dt.bfloat16, mybir.dt.int32, mybir.dt.uint32
RMAX, RADD = bass.bass_isa.ReduceOp.max, bass.bass_isa.ReduceOp.add

SLOPE = 0.01
EPS = 1e-5
ROWS = 1024
T = ROWS // P
COLS = 1024
B = COLS // P
HALF = T // 2
SCALE = 128.0
BY = [{"dve": (0,), "act": (1, 5, 6), "pool": (2, 3, 4, 7)},
      {"dve": (0, 4), "act": (1, 5, 6), "pool": (2, 3, 7)}]


def gat_layer(nc, x, adj, W, a, out):
    N, F = x.shape
    S = N // ROWS
    NB = N // P
    CH = N // COLS
    PAIRS = CH // 2
    F1 = F + 1
    GC = 2 * F1
    PER_BANK = 512 // GC
    SPANS = [(k, min(k + PER_BANK, T)) for k in range(0, T, PER_BANK)]
    AB = len(SPANS)
    STEPS = 2 * B
    assert F == 64 and N % ROWS == 0 and CH % 2 == 0 and 2 * AB + 2 == 8

    x_rows = x.rearrange("(s g p e) f -> s p g (e f)", p=P, g=2, e=HALF)
    out_rows = out.rearrange("(s g p e) f -> s p g (e f)", p=P, g=2, e=HALF)
    adj_halves = adj.rearrange("(s g p e) (c w) -> s c g p e w", p=P, g=2, e=HALF, w=COLS)

    TINY = 2.0 ** -100
    LIMITS = (6.0, 448.0 ** 2, NB * F / 64.0, 2.0 ** 98)

    with ExitStack() as ctx:
        def sb(name, shape, dt):
            return ctx.enter_context(nc.sbuf_tensor(name, shape, dt))

        def sem(name):
            return ctx.enter_context(nc.semaphore(name))

        acc = ctx.enter_context(nc.psum_tensor("acc", [P, 2 * AB, 512], F32))
        turned = ctx.enter_context(nc.psum_tensor("turned", [P, 2, ROWS], BF16))

        ring = sb("ring", [P, 4, HALF, COLS], I32)
        marks = sb("marks", [P, 2, T, COLS], BF16)
        signs = sb("signs", [P, 8, ROWS], BF16)
        edges = sb("edges", [P, 2, 4, ROWS], BF16)
        f1row = sb("f1row", [P, 2, ROWS], F32)
        f1col = sb("f1col", [P, T], F32)
        parts = sb("parts", [P, NB, 2, GC], F16)
        h = sb("h", [P, NB, F1], F32)
        f12 = sb("f12", [P, NB, 2], F32)
        f2tiny = sb("f2tiny", [P, NB], F32)
        a_in = sb("a_in", [F, 2], F32)
        ident16 = sb("ident16", [P, P], BF16)
        zeros = sb("zeros", [P, P], BF16)
        ones = sb("ones", [P, P], F32)
        ab = sb("ab", [P, 2, NB, 1], F32)
        stat = sb("stat", [P, 1], F32)
        bound = sb("bound", [P, 4], F32)
        squares = sb("squares", [P, CH], F32)
        bounds = sb("bounds", [P, 4], F32)
        beyond = sb("beyond", [P, 2], F32)
        flag = sb("flag", [P, 1], I32)
        fmax = sb("fmax", [P, 3], F32)
        hcol = sb("hcol", [P, 5, F1], F32)
        hsum = sb("hsum", [P, 1, F1], F32)
        sums = sb("sums", [P, 2, T, F1], F32)
        xin = sb("xin", [P, T, F], F32)
        dev = sb("dev", [P, T, F], F32)
        tiny = sb("tiny", [P, 6, T, 1], F32)

        pos, neg = edges[:, 0], edges[:, 1]
        x_all = edges[:].rearrange("p k a w -> p (k a w)").bitcast(F32).rearrange("p (g e f) -> p g e f", e=HALF, f=F)
        wt2 = sb("wt2", [F, 2, F], F32)
        wblk = sb("wblk", [P, 2, F + 2], F32)
        w_in = sb("w_in", [P, F], F32)
        ident = sb("ident", [P, P], F32)
        q = sb("q", [P, 2, NB], F32)
        z = sb("z", [P, 2, NB], F32)
        wide = sums
        alone, recip, mean, var, rstd, work = (tiny[:, i] for i in range(6))
        xT = parts[:].rearrange("p t k c -> p (t k c)")[:, 0:NB * F * 2].bitcast(F32)

        x_loaded, w_loaded, a_loaded = sem("x_loaded"), sem("w_loaded"), sem("a_loaded")
        adj_loaded = [sem(f"adj_loaded{i}") for i in range(4)]
        marked = {e: sem(f"marked_{e}") for e in ("dve", "act", "pool")}
        consts_ready, w_placed = sem("consts_ready"), sem("w_placed")
        product_made = sem("product_made")
        product_taken = {"dve": sem("product_taken_dve"), "act": sem("product_taken_act")}
        stat_ready, fmax_ready, shift_ready = sem("stat_ready"), sem("fmax_ready"), sem("shift_ready")
        q_ready, q_scaled, z_ready, ab_ready = sem("q_ready"), sem("q_scaled"), sem("z_ready"), sem("ab_ready")
        parts_ready = {kind: sem(f"parts_ready{kind}") for kind in range(2)}
        f1col_ready, f1row_made, f1row_taken = sem("f1col_ready"), sem("f1row_made"), sem("f1row_taken")
        f2tiny_ready, squares_ready = sem("f2tiny_ready"), sem("squares_ready")
        hcol_ready, hsum_ready = sem("hcol_ready"), sem("hsum_ready")
        turned_done, signs_made = sem("turned_done"), sem("signs_made")
        edges_made, main_done = sem("edges_made"), sem("main_done")
        acc_taken, agg_ready, recip_ready = sem("acc_taken"), sem("agg_ready"), sem("recip_ready")
        xin_loaded, ratio_ready, below_ready = sem("xin_loaded"), sem("ratio_ready"), sem("below_ready")
        above_ready, exp_ready = sem("above_ready"), sem("exp_ready")
        y_ready, seed_ready = sem("y_ready"), sem("seed_ready")
        out_ready, dev_free = sem("out_ready"), sem("dev_free")
        last_out = sem("last_out")
        bound_ready, bounds_ready, flag_ready = sem("bound_ready"), sem("bounds_ready"), sem("flag_ready")
        g_adj_loaded, g_x_loaded, g_stored, g_row_made, g_row_taken = (
            sem(n) for n in ("g_adj_loaded", "g_x_loaded", "g_stored", "g_row_made", "g_row_taken"))
        g_scored, g_masked, g_weighted, g_turns, g_copied, g_added = (
            sem(n) for n in ("g_scored", "g_masked", "g_weighted", "g_turns", "g_copied", "g_added"))
        g_below_ready, g_exp_ready, g_out_ready, g_dve_own = (
            sem(n) for n in ("g_below_ready", "g_exp_ready", "g_out_ready", "g_dve_own"))
        dve_own, pool_own = sem("dve_own"), sem("pool_own")
        var_chain, high_taken = sem("var_chain"), sem("high_taken")

        passed = {nc.sync: sem("passed_sync"), nc.scalar: sem("passed_scalar"), nc.vector: sem("passed_vector"),
                  nc.gpsimd: sem("passed_gpsimd"), nc.tensor: sem("passed_tensor")}

        def flat(rows):
            return rows[:].rearrange("p (g e) f -> p g (e f)", e=HALF)

        def hold(eng, signal, value):
            eng.wait_ge(signal, value).then_inc(passed[eng], 1)

        def at(kind, k):
            return acc[:, AB * kind + k // PER_BANK, GC * (k % PER_BANK):GC * (k % PER_BANK + 1)]

        products = [("wt", 0), ("wa", 0)] + [("xt", g) for g in range(NB // 8)] \
            + [("h", g) for g in range(NB // 4)] + [("f1", g) for g in range(4)]
        number = {p: n for n, p in enumerate(products)}
        BANKS = 2 * AB
        LEAVING = (BANKS - 2, BANKS - 1, *range(BANKS - 2))

        def taken(eng, n):
            eng.wait_ge(product_taken["act" if n % 2 else "dve"], n // 2 + 1)

        def take_products(eng, engine, copy):
            for n, (what, g) in enumerate(products):
                if ("act" if n % 2 else "dve") != engine:
                    continue
                bank = acc[:, n % BANKS]
                eng.wait_ge(product_made, n + 1)
                if what == "wt":
                    copy(wt2[:, 0], bank[0:F, 0:F])
                    last = copy(wt2[:, 1], bank[0:F, 0:F])
                elif what == "wa":
                    for r in range(2):
                        rows = slice(F * r, F * r + F)
                        last = copy(wblk[rows, r, F:F + 2], bank[rows, 0:2])
                elif what == "xt":
                    last = copy(xT[:, 4 * P * g:4 * P * (g + 1)], bank)
                elif what == "h":
                    rows = bank[:, 0:4 * (F + 2)].rearrange("p (t f) -> p t f", f=F + 2)
                    copy(h[:, 4 * g:4 * g + 4, 0:F], rows[:, :, 0:F])
                    last = copy(f12[:, 4 * g:4 * g + 4, :], rows[:, :, F:F + 2])
                else:
                    last = copy(f1row[:, g // 2, 512 * (g % 2):512 * (g % 2 + 1)], bank)
                last.then_inc(product_taken[engine], 1)
                yield what, g

        def edges_marked(eng, pairs, chunks, tiles=0):
            for name in marked:
                shares = [BY[c % 2][name] for c in range(chunks + 2)]
                more = sum(len(shares[c]) for c in range(chunks)) + sum(k < tiles for k in shares[chunks])
                count = pairs * (len(shares[0]) + len(shares[1])) + more
                if isinstance(count, int):
                    eng.wait_ge(marked[name], count)
                else:
                    hold(eng, marked[name], count)

        def may_mark(eng, s, c, k):
            hold(eng, adj_loaded[2 * (c % 2) + k // HALF], (s * CH + c - c % 2) * 8 + 16)
            if not (isinstance(s, int) and s == 0 and c < 2):
                hold(eng, turned_done, (s * CH + c - 1) * B)

        def tile_of(c, k):
            return ring[:, 2 * (c % 2) + k // HALF, k % HALF], marks[:, c % 2, k]

        def columns(b):
            first = P * HALF * (b // HALF) + b % HALF
            return slice(first, first + HALF * (P - 1) + 1, HALF)

        def over_supers(eng, one):
            one(0, True, False)
            with eng.Fori(1, S - 1) as s:
                one(s, False, False)
            one(S - 1, False, True)

        def weigh(e, link, kind, c):
            blocks = slice(B * c, B * c + B)
            w = q[:, kind, blocks].rearrange("p (t o) -> p t o", o=1).to_broadcast([P, B, F1])
            high, low = parts[:, blocks, kind, 0:F1], parts[:, blocks, kind, F1:GC]
            if e is nc.gpsimd:
                e.tensor_tensor(wide[:, kind], h[:, blocks], w, ALU.mult)
                link(e.tensor_tensor(high, h[:, blocks], w, ALU.mult))
            else:
                link(e.tensor_tensor(wide[:, kind], h[:, blocks], w, ALU.mult))
                link(e.tensor_copy(high, wide[:, kind]))
            return e.tensor_tensor(low, wide[:, kind], high, ALU.subtract)

        def aggregate(e, link, s):
            for kind in range(2):
                last = e.tensor_tensor(sums[:, kind], sums[:, kind],
                                       ab[:, kind, bass.ds(s * T, T)].to_broadcast([P, T, F1]), ALU.mult)
            link(last)
            link(e.tensor_tensor(sums[:, 0], sums[:, 0], sums[:, 1], ALU.add))
            link(e.tensor_scalar(alone, sums[:, 0, :, F:F1], 0.0, None, ALU.is_le))
            link(e.tensor_tensor(sums[:, 1], hsum[:].to_broadcast([P, T, F1]), alone.to_broadcast([P, T, F1]), ALU.mult))
            return e.tensor_tensor(sums[:, 0], sums[:, 0], sums[:, 1], ALU.add)

        def ratio(e):
            return e.tensor_tensor(num, num, recip.to_broadcast([P, T, F]), ALU.mult)

        def split():
            nc.vector.tensor_scalar(below, num, 0.0, None, ALU.min).then_inc(below_ready, 1)
            nc.vector.tensor_scalar(num, num, 0.0, -1.0, ALU.max, ALU.add).then_inc(above_ready, 1)

        def spread(link):
            def minus_mean():
                link(nc.vector.tensor_reduce(mean, xin[:], AX_X, ALU.add))
                return nc.vector.tensor_scalar(mean, mean, -1.0 / F, None, ALU.mult)

            return [minus_mean, lambda: nc.vector.tensor_tensor(dev[:], xin[:], mean.to_broadcast([P, T, F]), ALU.add),
                    lambda: nc.vector.tensor_tensor(below, dev[:], dev[:], ALU.mult),
                    lambda: nc.vector.tensor_reduce(var, below, AX_X, ALU.add),
                    lambda: seed(link, var, rstd)]

        def seed(link, v, r):
            link(nc.vector.tensor_scalar(v, v, 1.0 / F, EPS, ALU.mult, ALU.add))
            link(nc.vector.tensor_scalar(r.bitcast(I32), v.bitcast(I32), 1, None, ALU.logical_shift_right))
            return nc.vector.tensor_scalar(r.bitcast(I32), r.bitcast(I32), -1.0, float(0x5F3759DF), ALU.mult, ALU.add)

        def newton(e, link, v, r, t):
            for _ in range(3):
                link(e.tensor_tensor(t, r, r, ALU.mult))
                link(e.tensor_tensor(t, t, v, ALU.mult))
                link(e.tensor_scalar(t, t, -0.5, 1.5, ALU.mult, ALU.add))
                link(e.tensor_tensor(r, r, t, ALU.mult))

        def normed(e):
            return e.tensor_tensor(dev[:], dev[:], rstd.to_broadcast([P, T, F]), ALU.mult)

        halves = ring[:].rearrange("p (a b) t w -> p a (b t w)", a=2)
        g_adj, g_scores = halves[:, 0], halves[:, 1].bitcast(F32)
        g_f2row = marks[:].rearrange("p a t w -> p (a t w)").bitcast(F32)
        g_mask = pos.rearrange("p a w -> p (a w)").bitcast(F32)
        g_turned = neg.rearrange("p a w -> p (a w)").bitcast(F32).rearrange("p (g w) -> p g w", g=4)
        g_h, g_below, g_sq, g_dev, g_x = sums[:, 0, 0, 0:F], sums[:, 0, 1, 0:F], sums[:, 0, 2, 0:F], dev[:, 0], xin[:, 0]
        g_max, g_sum, g_recip, g_mean, g_var, g_rstd = (sums[:, 1, i, 0:1] for i in range(6))

        num, below = sums[:, 0, :, 0:F], sums[:, 1, :, 0:F]

        def where_needed(eng, general):
            eng.wait_ge(flag_ready, 1)
            with eng.If(eng.value_load(flag[0:1, 0:1], min_val=0, max_val=1) > 0):
                general()

        block = ctx.enter_context(nc.Block())

        @block.sync
        def _(sp):
            def load(s, c):
                for half in range(2):
                    edges_marked(sp, s * PAIRS + (c - 2) // 2, c % 2, (half + 1) * HALF)
                    src = adj_halves[bass.ds(s, 1), c, half].rearrange("s p e w -> p (s e) w")
                    sp.dma_start(ring[:, 2 * (c % 2) + half], src).then_inc(adj_loaded[2 * (c % 2) + half], 16)

            def rows_in(s):
                if not (isinstance(s, int) and s == 0):
                    hold(sp, out_ready, s)
                sp.dma_start(flat(xin), x_rows[bass.ds(s, 1)].rearrange("s p g w -> p (s g) w")).then_inc(xin_loaded, 16)

            sp.dma_start(w_in[0:F, :], W).then_inc(w_loaded, 16)
            sp.dma_start(w_in[F:2 * F, :], W).then_inc(w_loaded, 16)
            with nc.allow_non_contiguous_dma(reason="128 numbers"):
                sp.dma_start(a_in[:, :], a.rearrange("(c f) o -> f (c o)", c=2)).then_inc(a_loaded, 16)
            sp.dma_start(x_all.rearrange("p g e f -> p g (e f)"), x.rearrange("(g p e) f -> p g (e f)", p=P, e=HALF)) \
                .then_inc(x_loaded, 16)
            for c in range(2):
                for half in range(2):
                    sp.dma_start(ring[:, 2 * c + half], adj_halves[0, c, half]).then_inc(adj_loaded[2 * c + half], 16)

            def one(s, first, last):
                for c in range(CH):
                    if not first or c > 1:
                        load(s, c)
                    if c == 2 and not first:
                        rows_in(s - 1)

            over_supers(sp, one)
            rows_in(S - 1)
            sp.wait_ge(last_out, 1)
            sp.dma_start(out_rows[S - 1], flat(dev)).then_inc(dev_free, 16)
            sp.wait_ge(dev_free, 16 * (S + 1))

            def general():
                rows_of = [v.rearrange("(g p e) c -> g p e c", p=P, e=HALF) for v in (adj, x, out)]
                with sp.Fori(0, NB // HALF) as g:
                    with sp.Fori(0, HALF) as e:
                        t = g * HALF + e
                        adj_rows, x_rows, out_rows = (
                            v[bass.ds(g, 1), :, bass.ds(e, 1)].rearrange("g p e c -> p (g e c)") for v in rows_of)
                        sp.dma_start(g_adj, adj_rows).then_inc(g_adj_loaded, 16)
                        sp.dma_start(g_x, x_rows).then_inc(g_x_loaded, 16)
                        hold(sp, g_out_ready, t + 1)
                        sp.dma_start(out_rows, g_dev).then_inc(g_stored, 16)
                        hold(sp, g_stored, t * 16 + 16)

            where_needed(sp, general)

        @block.gpsimd
        def _(pool):
            nc.gpsimd.memset(ident[:], 0.0).then_inc(pool_own, 1)
            pool.wait_ge(pool_own, 1)
            nc.gpsimd.affine_select(out=ident[:], in_=ident[:], compare_op=ALU.not_equal, fill=1.0, base=0,
                                    pattern=[[-1, P]], channel_multiplier=1).then_inc(pool_own, 1)
            pool.wait_ge(pool_own, 2)
            nc.gpsimd.tensor_copy(ident16[:], ident[:])
            nc.gpsimd.memset(wblk[:], 0.0)
            nc.gpsimd.memset(ones[:], 1.0)
            nc.gpsimd.memset(zeros[:].bitcast(F32), 0.0)
            nc.gpsimd.memset(h[:, :, F:F1], 1.0).then_inc(consts_ready, 1)

            def mark(s, c, tiles=range(T)):
                for k in (k for k in BY[c % 2]["pool"] if k in tiles):
                    may_mark(pool, s, c, k)
                    src, dst = tile_of(c, k)
                    nc.gpsimd.tensor_scalar(dst, src, 0, None, ALU.is_le).then_inc(marked["pool"], 1)

            def static_link(ins):
                own[0] += 1
                ins.then_inc(pool_own, 1)
                pool.wait_ge(pool_own, own[0])

            own = [2]
            mark(0, 0, (2, 3, 4))
            pool.wait_ge(stat_ready, 1)
            nc.gpsimd.partition_all_reduce(fmax[:, 0:1], stat[:], P, RMAX).then_inc(fmax_ready, 1)
            mark(0, 0, (7,))
            mark(0, 1)
            pool.wait_ge(q_scaled, 1)

            LINKS = 4 + 1 + 12

            def one(s, first, last):
                count = [0]

                def link(ins):
                    count[0] += 1
                    ins.then_inc(pool_own, 1)
                    hold(pool, pool_own, (s - 1) * LINKS + (own[0] + count[0]))

                for c in range(CH):
                    if first and c + 1 < CH:
                        pool.wait_ge(parts_ready[1], c + 1)
                        weigh(nc.gpsimd, static_link, 1, c + 1).then_inc(parts_ready[1], 1)
                    if not (last and c == CH - 1) and not (first and c == 0):
                        mark(s + (c + 1) // CH, (c + 1) % CH)
                    if first and c == 5:
                        pool.wait_ge(hcol_ready, 5)
                        nc.gpsimd.partition_all_reduce(hsum[:, 0], hcol[:, 4], P, RADD).then_inc(hsum_ready, 1)
                    if first:
                        continue
                    if c == 0:
                        hold(pool, acc_taken, s * BANKS)
                        pool.wait_ge(ab_ready, 1)
                        pool.wait_ge(hsum_ready, 1)
                        aggregate(nc.gpsimd, link, s - 1).then_inc(agg_ready, 1)
                    if c == 2:
                        hold(pool, recip_ready, s)
                        ratio(nc.gpsimd).then_inc(ratio_ready, 1)
                    if c == 4:
                        hold(pool, xin_loaded, s * 16)
                        hold(pool, above_ready, s)
                        link(nc.gpsimd.tensor_tensor(xin[:], xin[:], num, ALU.add))
                        hold(pool, exp_ready, s)
                        nc.gpsimd.tensor_tensor(xin[:], xin[:], below, ALU.add).then_inc(y_ready, 1)
                    if c == 6:
                        hold(pool, seed_ready, s)
                        newton(nc.gpsimd, link, var, rstd, work)
                        normed(nc.gpsimd).then_inc(out_ready, 1)
                assert first or count[0] == LINKS

            over_supers(pool, one)
            pool.wait_ge(bound_ready, 2)
            nc.gpsimd.partition_all_reduce(bounds[:], bound[:], P, RMAX).then_inc(bounds_ready, 1)

        @block.scalar
        def _(act):
            def copy(dst, src):
                return nc.scalar.copy(dst, src)

            act.wait_ge(consts_ready, 1)
            act.wait_ge(w_loaded, 32)
            for r in range(2):
                rows = slice(F * r, F * r + F)
                last = copy(wblk[rows, r, 0:F], w_in[rows, :])
            last.then_inc(w_placed, 1)
            def mark(s, c, k):
                may_mark(act, s, c, k)
                src, dst = tile_of(c, k)
                nc.scalar.activation(dst, src, ACT.Relu, bias=ones[:, 0:1], scale=-1.0).then_inc(marked["act"], 1)

            early = {("h", 3): [(0, 1)], ("f1", 3): [(0, 5), (0, 6)]}
            for product in take_products(act, "act", copy):
                for place in early.get(product, []):
                    mark(0, *place)
            act.wait_ge(shift_ready, 1)
            nc.scalar.activation(q[:, 0], f12[:, :, 1], ACT.Exp, bias=fmax[:, 1:2])
            nc.scalar.activation(q[:, 1], f12[:, :, 1], ACT.Exp, bias=fmax[:, 2:3], scale=SLOPE).then_inc(q_ready, 1)
            act.wait_ge(z_ready, 1)
            nc.scalar.activation(ab[:, :, :, 0], z[:], ACT.Exp).then_inc(ab_ready, 1)
            mark(0, 1, BY[1]["act"][0])

            act.wait_ge(f2tiny_ready, 1)
            for g in range(4):
                taken(act, number["f1", g])

            def sign(s, jb):
                n = s * NB + jb
                if not (isinstance(s, int) and s == 0 and jb < 8):
                    hold(act, edges_made, n * 2 - 14)
                row = f1row[:, bass.ds(s % 2, 1)].rearrange("p s w -> p (s w)")
                nc.scalar.activation(signs[:, jb % 8], row, ACT.Relu, bias=f2tiny[:, jb:jb + 1], scale=TINY) \
                    .then_inc(signs_made, 1)

            def next_f1(s):
                nc.scalar.copy(f1col[:], f12[:, bass.ds((s + 2) % S * T, T), 0:1].rearrange("p t o -> p (t o)")) \
                    .then_inc(f1col_ready, 1)

            def take_f1(s):
                for b in range(2):
                    hold(act, f1row_made, (s - 1) * 2 + b + 1)
                    nc.scalar.copy(f1row[:, bass.ds((s + 1) % 2, 1), 512 * b:512 * (b + 1)].rearrange("p s w -> p (s w)"),
                                   acc[:, LEAVING[b]]).then_inc(f1row_taken, 1)

            def exp_below(s):
                act.wait_ge(below_ready, s + 1)
                nc.scalar.activation(below, below, ACT.Exp).then_inc(exp_ready, 1)

            def rows_out(s):
                hold(act, out_ready, s + 1)
                act.dma_start(out_rows[bass.ds(s, 1)].rearrange("s p g w -> p (s g) w"), flat(dev)).then_inc(dev_free, 16)

            ACT_AT = [1, 3, 5, 7]

            def one(s, first, last):
                for c in range(CH):
                    if first:
                        if c:
                            act.wait_ge(squares_ready, c)
                        nc.scalar.activation(dev[:], h[:, B * c:B * c + B, 0:F], ACT.Square,
                                             accum_out=squares[:, c:c + 1]).then_inc(squares_ready, 1)
                    if c == 5 and not last:
                        next_f1(s)
                    for i in range(B):
                        sign(s, c * B + i)
                        if i == 4 and c == 0 and not first:
                            take_f1(s)
                        for k, when in zip(BY[(c + 1) % 2]["act"], ACT_AT):
                            if i == when and not (last and c == CH - 1) and not (first and c == 0 and i == ACT_AT[0]):
                                mark(s + (c + 1) // CH, (c + 1) % CH, k)
                    if c == CH - 1 and first:
                        act.wait_ge(squares_ready, CH).then_inc(dev_free, 16)
                    if c == 3 and not first:
                        exp_below(s - 1)
                    if c == 7 and not first:
                        rows_out(s - 1)

            over_supers(act, one)
            exp_below(S - 1)

            def general():
                act.wait_ge(g_row_taken, NB // 4)
                with act.Fori(0, NB) as t:
                    hold(act, g_adj_loaded, t * 16 + 16)
                    nc.scalar.activation(g_scores, g_f2row, ACT.Identity, bias=f12[:, bass.ds(t, 1), 0:1]
                                         .rearrange("p t o -> p (t o)")).then_inc(g_scored, 1)
                    hold(act, g_masked, t + 1)
                    nc.scalar.activation(g_scores, g_scores, ACT.Exp, bias=g_max, accum_out=g_sum).then_inc(g_weighted, 1)
                    hold(act, g_below_ready, t + 1)
                    nc.scalar.activation(g_below, g_below, ACT.Exp).then_inc(g_exp_ready, 1)

            where_needed(act, general)

        @block.vector
        def _(dve):
            own = [0]

            def link(ins):
                own[0] += 1
                ins.then_inc(dve_own, 1)
                dve.wait_ge(dve_own, own[0])

            def copy(dst, src):
                return nc.vector.tensor_copy(dst, src)

            def mark(s, c, k):
                may_mark(dve, s, c, k)
                src, dst = tile_of(c, k)
                nc.vector.tensor_scalar(dst, src, 0, None, ALU.is_le).then_inc(marked["dve"], 1)

            def quarter(i):
                for g in (4 * i + 2, 4 * i + 3):
                    taken(dve, number["h", g])
                nc.vector.tensor_reduce(hcol[:, i], h[:, NB // 4 * i:NB // 4 * (i + 1)].rearrange("p t f -> p f t"), AX_X,
                                        ALU.add).then_inc(hcol_ready, 1)

            early = {("h", 4): [(0, 0)]}
            for product in take_products(dve, "dve", copy):
                for place in early.get(product, []):
                    mark(0, *place)
                if product in (("h", 6), ("h", 10)):
                    quarter(product[1] // 4 - 1)
                if product == ("h", NB // 4 - 2):
                    for g in (NB // 4 - 2, NB // 4 - 1):
                        taken(dve, number[("h", g)])
                    nc.vector.reduce_max(stat[:], f12[:, :, 1], AX_X).then_inc(stat_ready, 1)
                    nc.vector.tensor_scalar(f2tiny[:], f12[:, :, 1], TINY, None, ALU.mult).then_inc(f2tiny_ready, 1)
                    nc.vector.reduce_max(bound[:, 3:4], f12[:, :, 0], AX_X)
                    nc.vector.tensor_reduce(bound[:, 1:2], f12[:, :, 1], AX_X, ALU.min)
                    dve.wait_ge(stat_ready, 1)
                    link(nc.vector.tensor_copy(bound[:, 0:1], stat[:]))
                    nc.vector.tensor_scalar(bound[:, 1:2], bound[:, 1:2], -1.0, None, ALU.mult).then_inc(bound_ready, 1)
            quarter(2)
            dve.wait_ge(fmax_ready, 1)
            nc.vector.tensor_scalar(fmax[:, 1:2], fmax[:, 0:1], -1.0, None, ALU.mult)
            nc.vector.tensor_scalar(fmax[:, 2:3], fmax[:, 0:1], -SLOPE, None, ALU.mult).then_inc(shift_ready, 1)
            link(nc.vector.tensor_scalar(z[:, 0], f12[:, :, 0], fmax[:, 0:1], 1.0 - SLOPE, ALU.add, ALU.mult))
            link(nc.vector.tensor_scalar(z[:, 1], z[:, 0], -1.0, 0.0, ALU.mult, ALU.min))
            nc.vector.tensor_scalar(z[:, 0], z[:, 0], 0.0, None, ALU.min).then_inc(z_ready, 1)
            quarter(3)
            dve.wait_ge(q_ready, 1)
            nc.vector.tensor_scalar(q[:], q[:], SCALE, None, ALU.mult).then_inc(q_scaled, 1)
            dve.wait_ge(q_scaled, 1)
            dve.wait_ge(product_made, len(products))
            for kind in range(2):
                weigh(nc.vector, link, kind, 0).then_inc(parts_ready[kind], 1)
            mark(0, 1, BY[1]["dve"][0])

            def step(s, jb):
                n = s * NB + jb
                dve.wait_ge(turned_done, n + 1)
                dve.wait_ge(signs_made, n + 1)
                if not (isinstance(s, int) and s == 0 and jb < 4):
                    dve.wait_ge(main_done, n - 3)
                nc.vector.tensor_tensor(pos[:, jb % 4], signs[:, jb % 8], turned[:, jb % 2], ALU.is_gt) \
                    .then_inc(edges_made, 1)
                nc.vector.tensor_tensor(neg[:, jb % 4], signs[:, jb % 8], turned[:, jb % 2], ALU.is_equal) \
                    .then_inc(edges_made, 1)

            def take_sums(s):
                dve.wait_ge(main_done, s * NB + NB)
                banks = [(b, b // AB, *SPANS[b % AB]) for b in LEAVING]
                for i in range(BANKS + 1):
                    if i < BANKS:
                        b, kind, k0, k1 = banks[i]
                        high = acc[:, b, 0:GC * (k1 - k0)].rearrange("p (k c) -> p k c", c=GC)[:, :, 0:F1]
                        copy(sums[:, kind, k0:k1], high).then_inc(high_taken, 1)
                    if i:
                        b, kind, k0, k1 = banks[i - 1]
                        low = acc[:, b, 0:GC * (k1 - k0)].rearrange("p (k c) -> p k c", c=GC)[:, :, F1:GC]
                        dve.wait_ge(high_taken, s * BANKS + i)
                        nc.vector.tensor_tensor(sums[:, kind, k0:k1], sums[:, kind, k0:k1], low, ALU.add) \
                            .then_inc(acc_taken, 1)

            def reciprocal(s):
                dve.wait_ge(agg_ready, s + 1)
                nc.vector.reciprocal(recip, sums[:, 0, :, F:F1]).then_inc(recip_ready, 1)

            def linked(chain, value, ins):
                ins.then_inc(chain, 1)
                dve.wait_ge(chain, value)

            DVE_AT = [1, 4]

            def one(s, first, last):
                for c in range(CH):
                    if c == 5 and not first:
                        count = [0]

                        def in_loop(ins):
                            count[0] += 1
                            linked(var_chain, (s - 1) * 7 + count[0], ins)

                        dve.wait_ge(y_ready, s)
                        dve.wait_ge(dev_free, s * 16)
                        pieces = spread(in_loop)
                    for i in range(B):
                        step(s, c * B + i)
                        if i == 3 and first and c + 1 < CH:
                            dve.wait_ge(parts_ready[0], c + 1)
                            weigh(nc.vector, link, 0, c + 1).then_inc(parts_ready[0], 1)
                        if c == 3 and i == 0 and not first:
                            dve.wait_ge(ratio_ready, s)
                            split()
                        if c == 5 and not first and i < len(pieces):
                            if i:
                                dve.wait_ge(var_chain, (s - 1) * 7 + count[0])
                            if i + 1 < len(pieces):
                                pieces[i]().then_inc(var_chain, 1)
                                count[0] += 1
                            else:
                                pieces[i]().then_inc(seed_ready, 1)
                                assert count[0] == 7
                        if c == 0 and i == 1 and not first:
                            take_sums(s - 1)
                        for k, when in zip(BY[(c + 1) % 2]["dve"], DVE_AT):
                            if i == when and not (last and c == CH - 1) and not (first and c == 0 and i == DVE_AT[0]):
                                mark(s + (c + 1) // CH, (c + 1) % CH, k)
                    if c == CH - 1 and first:
                        dve.wait_ge(squares_ready, CH)
                        nc.vector.reduce_sum(bound[:, 2:3], squares[:], AX_X).then_inc(bound_ready, 1)
                    if c == 4 and first:
                        dve.wait_ge(hcol_ready, 4)
                        nc.vector.tensor_reduce(hcol[:, 4], hcol[:, 0:4].rearrange("p t f -> p f t"), AX_X, ALU.add) \
                            .then_inc(hcol_ready, 1)
                    if c == 1 and not first:
                        reciprocal(s - 1)
            over_supers(dve, one)
            dve.wait_ge(bounds_ready, 1)
            link(nc.vector.tensor_tensor(beyond[:, 0:1], bounds[:, 0:1], bounds[:, 1:2], ALU.add))
            link(nc.vector.tensor_scalar(beyond[:, 0:1], beyond[:, 0:1], LIMITS[0], None, ALU.is_le))
            link(nc.vector.tensor_scalar(beyond[:, 1:2], bounds[:, 2:3], LIMITS[1], None, ALU.is_le))
            link(nc.vector.tensor_tensor(beyond[:, 0:1], beyond[:, 0:1], beyond[:, 1:2], ALU.mult))
            link(nc.vector.tensor_scalar(beyond[:, 1:2], bounds[:, 2:3], LIMITS[2], None, ALU.is_ge))
            link(nc.vector.tensor_tensor(beyond[:, 0:1], beyond[:, 0:1], beyond[:, 1:2], ALU.mult))
            link(nc.vector.tensor_tensor(beyond[:, 1:2], bounds[:, 0:1], bounds[:, 3:4], ALU.max))
            link(nc.vector.tensor_scalar(beyond[:, 1:2], beyond[:, 1:2], LIMITS[3], None, ALU.is_le))
            link(nc.vector.tensor_tensor(beyond[:, 0:1], beyond[:, 0:1], beyond[:, 1:2], ALU.mult))
            nc.vector.tensor_scalar(flag[:], beyond[:, 0:1], 0.0, None, ALU.is_equal).then_inc(flag_ready, 1)
            take_sums(S - 1)
            dve.wait_ge(acc_taken, S * BANKS)
            dve.wait_ge(hsum_ready, 1)
            dve.wait_ge(ab_ready, 1)
            link(aggregate(nc.vector, link, S - 1))
            link(nc.vector.reciprocal(recip, sums[:, 0, :, F:F1]))
            link(ratio(nc.vector))
            split()
            dve.wait_ge(above_ready, S)
            dve.wait_ge(xin_loaded, S * 16)
            link(nc.vector.tensor_tensor(xin[:], xin[:], num, ALU.add))
            dve.wait_ge(exp_ready, S)
            link(nc.vector.tensor_tensor(xin[:], xin[:], below, ALU.add))
            dve.wait_ge(dev_free, S * 16)
            for piece in spread(link):
                link(piece())
            newton(nc.vector, link, var, rstd, work)
            normed(nc.vector).then_inc(last_out, 1)
            def general():
                links = [0]

                def own(t, ins):
                    links[0] += 1
                    ins.then_inc(g_dve_own, 1)
                    dve.wait_ge(g_dve_own, t * OWN + links[0])

                for g in range(NB // 4):
                    dve.wait_ge(g_row_made, g + 1)
                    copy(g_f2row[:, 4 * P * g:4 * P * (g + 1)].rearrange("p (w e) -> p e w", e=HALF),
                         acc[:, g % 4].rearrange("p (e w) -> p e w", e=HALF)).then_inc(g_row_taken, 1)

                QUARTER = N // 4
                OWN = 3 * 4 + 11 + 3 + 12
                with dve.Fori(0, NB) as t:
                    dve.wait_ge(g_adj_loaded, t * 16 + 16)
                    dve.wait_ge(g_x_loaded, t * 16 + 16)
                    dve.wait_ge(g_scored, t + 1)
                    for i in range(4):
                        span = slice(QUARTER * i, QUARTER * (i + 1))
                        own(t, nc.vector.scalar_tensor_tensor(g_scores[:, span], g_scores[:, span], SLOPE,
                                                                      g_scores[:, span], ALU.mult, ALU.max))
                        nc.vector.scalar_tensor_tensor(g_scores[:, span], g_adj[:, span], 0.0, g_scores[:, span],
                                                       ALU.is_gt, ALU.mult)
                        own(t, nc.vector.tensor_scalar(g_mask, g_adj[:, span], 0.0, -1e12, ALU.is_le, ALU.mult))
                        own(t, nc.vector.tensor_tensor(g_scores[:, span], g_scores[:, span], g_mask, ALU.add))
                    own(t, nc.vector.reduce_max(g_max, g_scores, AX_X))
                    nc.vector.tensor_scalar(g_max, g_max, -1.0, None, ALU.mult).then_inc(g_masked, 1)
                    for g in range(NB // 4):
                        dve.wait_ge(g_turns, t * (NB // 4) + (g + 1))
                        copy(g_turned[:, g % 4], acc[:, g % 4]).then_inc(g_copied, 1)
                    dve.wait_ge(g_added, t + 1)
                    own(t, nc.vector.reciprocal(g_recip, g_sum))
                    own(t, nc.vector.tensor_scalar(g_h, acc[:, 5, 0:F], g_recip, None, ALU.mult))
                    nc.vector.tensor_scalar(g_below, g_h, 0.0, None, ALU.min).then_inc(g_below_ready, 1)
                    own(t, nc.vector.tensor_scalar(g_h, g_h, 0.0, -1.0, ALU.max, ALU.add))
                    own(t, nc.vector.tensor_tensor(g_h, g_h, g_x, ALU.add))
                    dve.wait_ge(g_exp_ready, t + 1)
                    own(t, nc.vector.tensor_tensor(g_h, g_h, g_below, ALU.add))
                    own(t, nc.vector.reduce_sum(g_mean, g_h, AX_X))
                    own(t, nc.vector.tensor_scalar(g_mean, g_mean, -1.0 / F, None, ALU.mult))
                    own(t, nc.vector.tensor_scalar(g_dev, g_h, g_mean, None, ALU.add))
                    own(t, nc.vector.tensor_tensor(g_sq, g_dev, g_dev, ALU.mult))
                    own(t, nc.vector.reduce_sum(g_var, g_sq, AX_X))
                    own(t, seed(lambda ins: own(t, ins), g_var, g_rstd))
                    newton(nc.vector, lambda ins: own(t, ins), g_var, g_rstd, g_mean)
                    nc.vector.tensor_scalar(g_dev, g_dev, g_rstd, None, ALU.mult).then_inc(g_out_ready, 1)
                assert links[0] == OWN

            where_needed(dve, general)

        @block.tensor
        def _(pe):
            def spread_f1(b, col):
                for i in range(4):
                    last = nc.tensor.matmul(acc[:, b, P * i:P * i + P], col[:, i:i + 1].to_broadcast([P, P]), ident[:],
                                            start=True, stop=True)
                return last

            pe.wait_ge(consts_ready, 1)
            pe.wait_ge(w_loaded, 32)
            for n, (what, g) in enumerate(products):
                bank = acc[:, n % BANKS]
                if n >= BANKS:
                    taken(pe, n - BANKS)
                if what == "wt":
                    last = nc.tensor.transpose(bank[0:F, 0:F], w_in[0:F, :], ident[0:F, 0:F])
                elif what == "wa":
                    taken(pe, number[("wt", 0)])
                    pe.wait_ge(a_loaded, 16)
                    last = nc.tensor.matmul(bank[:, 0:2], wt2[:].rearrange("f r k -> f (r k)"), a_in[:, :],
                                            start=True, stop=True)
                elif what == "xt":
                    pe.wait_ge(x_loaded, 16)
                    for i in range(4):
                        u = 4 * g + i
                        last = nc.tensor.transpose(bank[:, P * i:P * i + P],
                                                   x_all[:, u // 2, 2 * (u % 2):2 * (u % 2) + 2].rearrange("p e f -> p (e f)"), ident[:])
                elif what == "h":
                    taken(pe, number[("xt", g // 2)])
                    taken(pe, number[("wa", 0)])
                    pe.wait_ge(w_placed, 1)
                    for i in range(2):
                        last = nc.tensor.matmul(bank[:, 2 * (F + 2) * i:2 * (F + 2) * (i + 1)], xT[:, P * (2 * g + i):P * (2 * g + i + 1)],
                                                wblk[:].rearrange("p r f -> p (r f)"), start=True, stop=True)
                else:
                    taken(pe, number[("h", g)])
                    last = spread_f1(n % BANKS, f12[:, 4 * g:4 * g + 4, 0:1].rearrange("p t o -> p (t o)"))
                last.then_inc(product_made, 1)
            for n in range(len(products) - BANKS, len(products)):
                taken(pe, n)

            def turn(slot, b, place):
                for k in range(T):
                    last = nc.tensor.transpose(turned[:, place, P * k:P * k + P], marks[:, slot, k, columns(b)],
                                               ident16[:])
                last.then_inc(turned_done, 1)

            def zero(b):
                nc.tensor.matmul(acc[:, b].rearrange("p (o c) -> p o c", c=P), zeros[:],
                                 zeros[:].rearrange("p (o c) -> p o c", o=1).to_broadcast([P, 4, P]), start=True, stop=True)

            for b in range(BANKS):
                zero(b)
            edges_marked(pe, 0, 1)
            turn(0, 0, 0)
            turn(0, 1, 1)
            pe.wait_ge(edges_made, 2)
            turn(0, 2, 0)

            def pair(s, m, last):
                for i in range(STEPS):
                    if i % B == 0:
                        for kind in range(2):
                            pe.wait_ge(parts_ready[kind], m * 2 + (i // B + 1))
                    n = s * NB + (m * STEPS + i)
                    for kind, made in enumerate((pos, neg)):
                        weights = parts[:, bass.ds(m * STEPS + i, 1), kind].rearrange("p t c -> p (t c)")
                        for k in range(T):
                            ins = nc.tensor.matmul(at(kind, k), made[:, i % 4, P * k:P * k + P], weights,
                                                   start=False, stop=True, skip_group_check=True)
                    ins.then_inc(main_done, 1)
                    if not (last and i + 1 == STEPS):
                        pe.wait_ge(edges_made, n * 2 + 4)
                    ahead = i + 3
                    if not (last and ahead >= STEPS):
                        if ahead % B == 0:
                            edges_marked(pe, s * PAIRS + m, ahead // B + 1)
                        turn(ahead // B % 2, ahead % B, ahead % 2)

            with pe.Fori(0, S - 1) as s:
                with pe.Fori(0, PAIRS) as m:
                    pair(s, m, False)
                pe.wait_ge(f1col_ready, s + 1)
                for i, b in enumerate(LEAVING):
                    pe.wait_ge(acc_taken, s * BANKS + (i + 1))
                    if i < 2:
                        spread_f1(b, f1col[:, 4 * i:4 * i + 4]).then_inc(f1row_made, 1)
                    else:
                        zero(b)
                for i in range(2):
                    pe.wait_ge(f1row_taken, s * 2 + (i + 1))
                    zero(LEAVING[i])
            with pe.Fori(0, PAIRS - 1) as m:
                pair(S - 1, m, False)
            pair(S - 1, PAIRS - 1, True)

            def general():
                pe.wait_ge(last_out, 1)
                for g in range(NB // 4):
                    if g >= 4:
                        pe.wait_ge(g_row_taken, g - 3)
                    for i in range(4):
                        last = nc.tensor.matmul(acc[:, g % 4, P * i:P * i + P],
                                                f12[:, 4 * g + i, 1:2].to_broadcast([P, P]), ident[:], start=True, stop=True)
                    last.then_inc(g_row_made, 1)
                pe.wait_ge(g_row_taken, NB // 4)

                def turn_weights(g):
                    for i in range(4):
                        last = nc.tensor.transpose(acc[:, g % 4, P * i:P * i + P],
                                                   g_scores[:, columns(4 * g + i)], ident[:])
                    last.then_inc(g_turns, 1)

                with pe.Fori(0, NB) as t:
                    pe.wait_ge(g_weighted, t + 1)
                    turn_weights(0)
                    for g in range(NB // 4):
                        if g + 1 < NB // 4:
                            turn_weights(g + 1)
                        pe.wait_ge(g_copied, t * (NB // 4) + (g + 1))
                        for i in range(4):
                            last = nc.tensor.matmul(acc[:, 5, 0:F], g_turned[:, g % 4, P * i:P * i + P],
                                                    h[:, 4 * g + i, 0:F], start=(g == 0 and i == 0),
                                                    stop=(g == NB // 4 - 1 and i == 3))
                    last.then_inc(g_added, 1)

            where_needed(pe, general)


_INS = ["x", "adj", "L0_gnn_W", "L0_gnn_a"]


def kernel(**inputs):
    import numpy as _np
    import concourse.bacc as _bacc
    from concourse import mybir as _mybir
    from concourse.bass_utils import run_bass_kernel_spmd as _run

    nc = _bacc.Bacc("TRN2", target_bir_lowering=False, num_devices=1)
    arrays, args = {}, []
    for name in _INS:
        arr = _np.ascontiguousarray(inputs[name])
        arrays[f"in_{name}_dram"] = arr
        args.append(nc.dram_tensor(f"in_{name}_dram", arr.shape, _mybir.dt.from_np(arr.dtype), kind="ExternalInput").ap())
    out = nc.dram_tensor("out_0_dram", inputs["x"].shape, _mybir.dt.float32, kind="ExternalOutput").ap()
    gat_layer(nc, *args, out)
    return _run(nc, [arrays], core_ids=[0]).results[0]["out_0_dram"]
```
